# Optimizing a Trainium2 kernel written in Bass

```python
import numpy as np
import jax
import jax.numpy as jnp

def _softmax(x, axis=-1):
    return jax.nn.softmax(x, axis=axis)
def _gelu(x):
    return jax.nn.gelu(x, approximate=True)
def _silu(x):
    return jax.nn.silu(x)
def _sigmoid(x):
    return jax.nn.sigmoid(x)
def _layernorm(x, axis=-1, eps=1e-5):
    m = jnp.mean(x, axis=axis, keepdims=True)
    v = jnp.var(x, axis=axis, keepdims=True)
    return (x - m) / jnp.sqrt(v + eps)
def _scatter_add(tgt, idx, src, axis=0):
    return tgt.at[idx].add(src)
def _segment_sum(src, seg, n):
    return jax.ops.segment_sum(src, seg, n)

kernel_name = 'mk_conv_seq_d2_conv_nchw128_bf2295'

def setup_inputs(seed: int = 0):
    np.random.seed(seed)
    _w = jnp.asarray
    def _rec_inputs():
        import jax
        import jax.numpy as jnp
        _gk = jax.random.key(seed)
        x = -0.0005207 + 1.001 * jax.random.normal(jax.random.fold_in(_gk, 1), (4, 128, 64, 64), jnp.float32)
        return x
    x = _rec_inputs()
    def _L0_conv_setup():
        import jax, jax.numpy as jnp
        import numpy as np
        EPS = 1e-05
        key = jax.random.key(seed)
        ks = jax.random.split(key, 10)
        B, C, H, W = (4, 128, 64, 64)
        s = 1.0 / np.sqrt(C)
        return {'x': jax.random.normal(ks[0], (B, C, H, W), dtype=jnp.float32), 'Wq': jax.random.normal(ks[1], (C, C), dtype=jnp.float32) * s, 'bq': jax.random.normal(ks[2], (C,), dtype=jnp.float32) * 0.01, 'Wk': jax.random.normal(ks[3], (C, C), dtype=jnp.float32) * s, 'bk': jax.random.normal(ks[4], (C,), dtype=jnp.float32) * 0.01, 'Wv': jax.random.normal(ks[5], (C, C), dtype=jnp.float32) * s, 'bv': jax.random.normal(ks[6], (C,), dtype=jnp.float32) * 0.01, 'Wo': jax.random.normal(ks[7], (C, C), dtype=jnp.float32) * s, 'bo': jax.random.normal(ks[8], (C,), dtype=jnp.float32) * 0.01, 'gamma': jnp.ones((C,), dtype=jnp.float32), 'beta': jnp.zeros((C,), dtype=jnp.float32)}
    _L0_conv_all = _L0_conv_setup()
    _L0_conv_in = {k: v for k, v in _L0_conv_all.items() if k in ('Wq', 'bq', 'Wk', 'bk', 'Wv', 'bv', 'Wo', 'bo', 'gamma', 'beta', )}
    del _L0_conv_all

    def _L1_conv_setup():
        import jax, jax.numpy as jnp
        import numpy as np
        C = 128
        D_STATE = 16
        D_CONV = 4
        EXPAND = 2
        D_INNER = EXPAND * C
        DT_RANK = (C + 15) // 16
        B_SZ, H, W = (4, 64, 64)

        def _selective_scan(x, dt, A, B, Cm, D):
            b, l, d = x.shape

            def step(h, inp):
                xt, dtt, Bt, Ct = inp
                dA = jnp.exp(dtt[..., None] * A)
                h = dA * h + dtt[..., None] * Bt[:, None, :] * xt[..., None]
                y = jnp.einsum('bdn,bn->bd', h, Ct)
                return (h, y)
            h0 = jnp.zeros((b, d, A.shape[1]), x.dtype)
            xs = (x.transpose(1, 0, 2), dt.transpose(1, 0, 2), B.transpose(1, 0, 2), Cm.transpose(1, 0, 2))
            _, ys = jax.lax.scan(step, h0, xs)
            return ys.transpose(1, 0, 2) + x * D

        def _mamba(u, in_proj_w, conv1d_w, conv1d_b, x_proj_w, dt_proj_w, dt_proj_b, A_log, D, out_proj_w):
            xz = jnp.einsum('bld,ed->ble', u, in_proj_w)
            xi, z = jnp.split(xz, 2, axis=-1)
            xc = jax.lax.conv_general_dilated(xi.transpose(0, 2, 1), conv1d_w, (1,), ((D_CONV - 1, 0),), dimension_numbers=('NCH', 'OIH', 'NCH'), feature_group_count=D_INNER)
            xs = jax.nn.silu((xc + conv1d_b[None, :, None]).transpose(0, 2, 1))
            x_dbl = jnp.einsum('bld,rd->blr', xs, x_proj_w)
            dt = jax.nn.softplus(jnp.einsum('blr,dr->bld', x_dbl[..., :DT_RANK], dt_proj_w) + dt_proj_b)
            Bm = x_dbl[..., DT_RANK:DT_RANK + D_STATE]
            Cm = x_dbl[..., DT_RANK + D_STATE:]
            A = -jnp.exp(A_log)
            y = _selective_scan(xs, dt, A, Bm, Cm, D)
            y = y * jax.nn.silu(z)
            return jnp.einsum('bld,od->blo', y, out_proj_w)
        key = jax.random.key(seed)
        ks = jax.random.split(key, 12)
        n = lambda k, s, sc=0.02: jax.random.normal(k, s, dtype=jnp.float32) * sc
        return {'x': jax.random.normal(ks[0], (B_SZ, C, H, W), dtype=jnp.float32), 'conv_spatial_w': n(ks[1], (C, C, 3, 3)), 'conv_spatial_b': jnp.zeros((C,), jnp.float32), 'conv_spectral_w': n(ks[2], (2 * C, 2 * C, 1, 1)), 'conv_spectral_b': jnp.zeros((2 * C,), jnp.float32), 'in_proj_w': n(ks[3], (2 * D_INNER, C)), 'conv1d_w': n(ks[4], (D_INNER, 1, D_CONV), 0.2), 'conv1d_b': jnp.zeros((D_INNER,), jnp.float32), 'x_proj_w': n(ks[5], (DT_RANK + 2 * D_STATE, D_INNER)), 'dt_proj_w': n(ks[6], (D_INNER, DT_RANK), 0.1), 'dt_proj_b': n(ks[7], (D_INNER,), 0.1), 'A_log': jnp.log(jnp.broadcast_to(jnp.arange(1, D_STATE + 1, dtype=jnp.float32), (D_INNER, D_STATE))), 'D': jnp.ones((D_INNER,), jnp.float32), 'out_proj_w': n(ks[8], (C, D_INNER))}
    _L1_conv_all = _L1_conv_setup()
    _L1_conv_in = {k: v for k, v in _L1_conv_all.items() if k in ('conv_spatial_w', 'conv_spatial_b', 'conv_spectral_w', 'conv_spectral_b', 'in_proj_w', 'conv1d_w', 'conv1d_b', 'x_proj_w', 'dt_proj_w', 'dt_proj_b', 'A_log', 'D', 'out_proj_w', )}
    del _L1_conv_all

    return {
        "x": x,
        "L0_conv_Wq": _L0_conv_in["Wq"],
        "L0_conv_bq": _L0_conv_in["bq"],
        "L0_conv_Wk": _L0_conv_in["Wk"],
        "L0_conv_bk": _L0_conv_in["bk"],
        "L0_conv_Wv": _L0_conv_in["Wv"],
        "L0_conv_bv": _L0_conv_in["bv"],
        "L0_conv_Wo": _L0_conv_in["Wo"],
        "L0_conv_bo": _L0_conv_in["bo"],
        "L0_conv_gamma": _L0_conv_in["gamma"],
        "L0_conv_beta": _L0_conv_in["beta"],
        "L1_conv_conv_spatial_w": _L1_conv_in["conv_spatial_w"],
        "L1_conv_conv_spatial_b": _L1_conv_in["conv_spatial_b"],
        "L1_conv_conv_spectral_w": _L1_conv_in["conv_spectral_w"],
        "L1_conv_conv_spectral_b": _L1_conv_in["conv_spectral_b"],
        "L1_conv_in_proj_w": _L1_conv_in["in_proj_w"],
        "L1_conv_conv1d_w": _L1_conv_in["conv1d_w"],
        "L1_conv_conv1d_b": _L1_conv_in["conv1d_b"],
        "L1_conv_x_proj_w": _L1_conv_in["x_proj_w"],
        "L1_conv_dt_proj_w": _L1_conv_in["dt_proj_w"],
        "L1_conv_dt_proj_b": _L1_conv_in["dt_proj_b"],
        "L1_conv_A_log": _L1_conv_in["A_log"],
        "L1_conv_D": _L1_conv_in["D"],
        "L1_conv_out_proj_w": _L1_conv_in["out_proj_w"],
    }

def reference(x, L0_conv_Wq, L0_conv_bq, L0_conv_Wk, L0_conv_bk, L0_conv_Wv, L0_conv_bv, L0_conv_Wo, L0_conv_bo, L0_conv_gamma, L0_conv_beta, L1_conv_conv_spatial_w, L1_conv_conv_spatial_b, L1_conv_conv_spectral_w, L1_conv_conv_spectral_b, L1_conv_in_proj_w, L1_conv_conv1d_w, L1_conv_conv1d_b, L1_conv_x_proj_w, L1_conv_dt_proj_w, L1_conv_dt_proj_b, L1_conv_A_log, L1_conv_D, L1_conv_out_proj_w):
    import jax
    import jax.numpy as jnp
    def _L0_conv_ref(x, Wq, bq, Wk, bk, Wv, bv, Wo, bo, gamma, beta):
        import jax, jax.numpy as jnp
        import numpy as np
        EPS = 1e-05
        B, C, H, W = x.shape
        num_heads = 4
        head_dim = C // num_heads
        scale = head_dim ** (-0.5)
        x_flat = x.reshape(B, C, H * W).transpose(0, 2, 1)

        def split_heads(t):
            return t.reshape(B, H * W, num_heads, head_dim).transpose(0, 2, 1, 3)
        Q = split_heads(x_flat @ Wq + bq)
        K = split_heads(x_flat @ Wk + bk)
        V = split_heads(x_flat @ Wv + bv)
        attn = jax.nn.softmax(jnp.einsum('bhnd,bhmd->bhnm', Q, K) * scale, axis=-1)
        out = jnp.einsum('bhnm,bhmd->bhnd', attn, V)
        out = out.transpose(0, 2, 1, 3).reshape(B, H * W, C)
        out = out @ Wo + bo
        y = out + x_flat
        mu = jnp.mean(y, axis=-1, keepdims=True)
        var = jnp.mean(jnp.square(y - mu), axis=-1, keepdims=True)
        y = (y - mu) / jnp.sqrt(var + EPS) * gamma + beta
        return y.transpose(0, 2, 1).reshape(B, C, H, W)

    def _L1_conv_ref(x, conv_spatial_w, conv_spatial_b, conv_spectral_w, conv_spectral_b, in_proj_w, conv1d_w, conv1d_b, x_proj_w, dt_proj_w, dt_proj_b, A_log, D, out_proj_w):
        import jax, jax.numpy as jnp
        import numpy as np
        C = 128
        D_STATE = 16
        D_CONV = 4
        EXPAND = 2
        D_INNER = EXPAND * C
        DT_RANK = (C + 15) // 16
        B_SZ, H, W = (4, 64, 64)

        def _selective_scan(x, dt, A, B, Cm, D):
            b, l, d = x.shape

            def step(h, inp):
                xt, dtt, Bt, Ct = inp
                dA = jnp.exp(dtt[..., None] * A)
                h = dA * h + dtt[..., None] * Bt[:, None, :] * xt[..., None]
                y = jnp.einsum('bdn,bn->bd', h, Ct)
                return (h, y)
            h0 = jnp.zeros((b, d, A.shape[1]), x.dtype)
            xs = (x.transpose(1, 0, 2), dt.transpose(1, 0, 2), B.transpose(1, 0, 2), Cm.transpose(1, 0, 2))
            _, ys = jax.lax.scan(step, h0, xs)
            return ys.transpose(1, 0, 2) + x * D

        def _mamba(u, in_proj_w, conv1d_w, conv1d_b, x_proj_w, dt_proj_w, dt_proj_b, A_log, D, out_proj_w):
            xz = jnp.einsum('bld,ed->ble', u, in_proj_w)
            xi, z = jnp.split(xz, 2, axis=-1)
            xc = jax.lax.conv_general_dilated(xi.transpose(0, 2, 1), conv1d_w, (1,), ((D_CONV - 1, 0),), dimension_numbers=('NCH', 'OIH', 'NCH'), feature_group_count=D_INNER)
            xs = jax.nn.silu((xc + conv1d_b[None, :, None]).transpose(0, 2, 1))
            x_dbl = jnp.einsum('bld,rd->blr', xs, x_proj_w)
            dt = jax.nn.softplus(jnp.einsum('blr,dr->bld', x_dbl[..., :DT_RANK], dt_proj_w) + dt_proj_b)
            Bm = x_dbl[..., DT_RANK:DT_RANK + D_STATE]
            Cm = x_dbl[..., DT_RANK + D_STATE:]
            A = -jnp.exp(A_log)
            y = _selective_scan(xs, dt, A, Bm, Cm, D)
            y = y * jax.nn.silu(z)
            return jnp.einsum('bld,od->blo', y, out_proj_w)
        b, c, h, w = x.shape
        spatial = jax.lax.conv_general_dilated(x, conv_spatial_w, (1, 1), ((1, 1), (1, 1)), dimension_numbers=('NCHW', 'OIHW', 'NCHW')) + conv_spatial_b[None, :, None, None]
        u = x.transpose(0, 2, 3, 1).reshape(b, h * w, c)
        ym = _mamba(u, in_proj_w, conv1d_w, conv1d_b, x_proj_w, dt_proj_w, dt_proj_b, A_log, D, out_proj_w)
        ym = ym.reshape(b, h, w, c).transpose(0, 3, 1, 2)
        fft = jnp.fft.rfft2(x, axes=(-2, -1))
        cat = jnp.concatenate([fft.real, fft.imag], axis=1)
        fc = jnp.einsum('bchw,oc->bohw', cat, conv_spectral_w[:, :, 0, 0]) + conv_spectral_b[None, :, None, None]
        fr, fi = jnp.split(fc, 2, axis=1)
        spectral = jnp.fft.irfft2(jax.lax.complex(fr, fi), s=(h, w), axes=(-2, -1))
        return spatial + spectral + ym

    def _gn(v, G=32, eps=1e-5):
        B_, C_, H_, W_ = v.shape
        g = v.reshape(B_, G, C_ // G, H_, W_)
        m = jnp.mean(g, axis=(2, 3, 4), keepdims=True)
        s = jnp.var(g, axis=(2, 3, 4), keepdims=True)
        return ((g - m) / jnp.sqrt(s + eps)).reshape(v.shape)

    def _ln_c(v, eps=1e-6):
        m = jnp.mean(v, axis=1, keepdims=True)
        s = jnp.var(v, axis=1, keepdims=True)
        return (v - m) / jnp.sqrt(s + eps)

    def _ln_t(v, eps=1e-5):
        m = jnp.mean(v, axis=-1, keepdims=True)
        s = jnp.var(v, axis=-1, keepdims=True)
        return (v - m) / jnp.sqrt(s + eps)

    def _to_tokens(v):
        B_, C_, H_, W_ = v.shape
        return v.reshape(B_, C_, H_ * W_).transpose(0, 2, 1)
    def _from_tokens(t, like):
        B_, C_, H_, W_ = like.shape
        return t.transpose(0, 2, 1).reshape(B_, C_, H_, W_)

    x = _L0_conv_ref(x, L0_conv_Wq, L0_conv_bq, L0_conv_Wk, L0_conv_bk, L0_conv_Wv, L0_conv_bv, L0_conv_Wo, L0_conv_bo, L0_conv_gamma, L0_conv_beta)
    x = _L1_conv_ref(x, L1_conv_conv_spatial_w, L1_conv_conv_spatial_b, L1_conv_conv_spectral_w, L1_conv_conv_spectral_b, L1_conv_in_proj_w, L1_conv_conv1d_w, L1_conv_conv1d_b, L1_conv_x_proj_w, L1_conv_dt_proj_w, L1_conv_dt_proj_b, L1_conv_A_log, L1_conv_D, L1_conv_out_proj_w)
    return x


_drawn_inputs = setup_inputs


def setup_inputs(seed=0):
    import zlib

    import numpy as np

    out = dict(_drawn_inputs(seed))
    spreads = {'L0_conv_gamma': (1.0, 0.2),
     'L0_conv_beta': (0.0, 0.1),
     'L1_conv_conv_spatial_b': (0.0, 0.1),
     'L1_conv_conv_spectral_b': (0.0, 0.1),
     'L1_conv_conv1d_b': (0.0, 0.1),
     'L1_conv_D': (1.0, 0.2)}
    factors = {}
    for name, (base, spread) in spreads.items():
        noise = np.random.default_rng([zlib.crc32(name.encode()), seed]).standard_normal(out[name].shape)
        drawn = base * np.exp(spread * noise) if base else spread * noise
        out[name] = jnp.asarray(drawn.astype(out[name].dtype))
    for name, factor in factors.items():
        out[name] = (out[name] * factor).astype(out[name].dtype)
    return out
```

```python
import numpy as np
import concourse.bass as bass
import concourse.mybir as mybir
from contextlib import ExitStack

F32, F32R = mybir.dt.float32, mybir.dt.float32r
ACT = mybir.ActivationFunctionType
ALU = mybir.AluOpType
AX = mybir.AxisListType

B, C, H, W = 4, 128, 64, 64
L = H * W
HEADS = 4
D = C // HEADS
SCALE = D ** -0.5
CH = 512
NCH = L // CH
NT = L // 128
PAIRS = NT // 2
LN_EPS = 1e-5
PARTS = 3 * D
SHIFT = PARTS + 2


def pipelined(e, n, depth, emit):
    lead = depth - 1 + (depth - 1) % 2
    for step in range(lead):
        emit(step, step % 2, [s for s in range(depth) if 0 <= step - s < n])
    with e.Fori(lead // 2, n // 2) as k:
        for r in range(2):
            emit(k * 2 + r, r, list(range(depth)))
    for step in range(n, n + depth - 1):
        emit(step, step % 2, [s for s in range(depth) if 0 <= step - s < n])


def clear(nc, sems):
    with nc.Block() as block:
        @block.vector
        def _(dve):
            for s in sems:
                dve.sem_clear(s)


def layer0(nc, x, w, z_ext, z_flip, nb=B):
    qk_split = nc.dram_tensor("qk_split", [2, 2, C, L], F32, kind="Internal").ap()
    with ExitStack() as ctx:
        def sb(name, shape, dt=F32):
            return ctx.enter_context(nc.sbuf_tensor(name, shape, dt))

        names = []

        def sem(name):
            s = ctx.enter_context(nc.semaphore(name))
            names.append(s)
            return s

        ps = ctx.enter_context(nc.psum_tensor("ps", [128, 8, CH], F32))
        w_sb = sb("w_sb", [C, 4, C])
        bias = sb("bias", [C, 5])
        bv_sb = sb("bv_sb", [128, C])
        id_sb = sb("id_sb", [128, 128])
        ones_c = sb("ones_c", [C, C])
        sel_o = sb("sel_o", [128, D])
        sel_d = sb("sel_d", [128, D])
        eps = sb("eps", [128, 1])
        q_st = sb("q_st", [128, 2, L], F32R)
        k_st = sb("k_st", [128, 2, L], F32R)
        v_cur = sb("v_cur", [128, HEADS, NT, D + 1])
        v_next = sb("v_next", [128, HEADS, NT, D + 1])
        exps = sb("exps", [128, 4, 2 * CH])
        heads_out = sb("heads_out", [128, HEADS, L])
        mpart = sb("mpart", [128, NCH, NT])
        mneg = sb("mneg", [128, NT])
        mrow = sb("mrow", [NT, 2, 128], F32R)
        split_buf = sb("split_buf", [128, 2, 2, 2, CH], F32R)

        def work(i):
            if i < 8:
                return exps[:, i // 2, CH * (i % 2):CH * (i % 2) + CH]
            i -= 8
            return split_buf[:, i // 4, i // 2 % 2, i % 2, :].bitcast(F32)

        loaded = sem("loaded")
        made = sem("made")
        zero_ready = sem("zero_ready")

        with nc.Block() as block:
            @block.sync
            def _(sp):
                for i, name in enumerate(("Wq", "Wk", "Wv", "Wo")):
                    sp.dma_start(w_sb[:, i, :], w[name]).then_inc(loaded, 16)
                for i, name in enumerate(("bq", "bk", "bo", "gamma", "beta")):
                    sp.dma_start(bias[:, i:i + 1], w[name].rearrange("(c o) -> c o", o=1)).then_inc(loaded, 16)
                sp.dma_start(bv_sb[:, :], w["bv"].rearrange("(o c) -> o c", o=1).to_broadcast([128, C])).then_inc(loaded, 16)
                sp.dma_start(id_sb[:, :], w["ident"]).then_inc(loaded, 16)
                sp.wait_ge(zero_ready, 1)
                for b in range(B):
                    for at in (0, W + L):
                        sp.dma_start(z_ext[b, :, at:at + W], heads_out[:, 0, 0:W]).then_inc(loaded, 16)
                sp.wait_ge(loaded, 16 * (11 + 2 * B))

            @block.gpsimd
            def _(pool):
                pool.memset(heads_out[:, 0, 0:W], 0.0).then_inc(zero_ready, 1)
                pool.memset(v_next[:, :, :, D:D + 1], 1.0)
                pool.memset(v_cur[:, :, :, D:D + 1], 1.0)
                pool.memset(eps[:, :], LN_EPS)
                pool.memset(ones_c[:, :], 1.0 / C)

            @block.vector
            def _(dve):
                for buf in range(2):
                    nc.vector.memset(k_st[PARTS:128, buf, :].bitcast(F32), 1.0)
                nc.vector.memset(ps[:, 6:8, :], 0.0)
                nc.vector.memset(sel_o[:, :], 0.0).then_inc(made, 1)
                nc.vector.memset(sel_d[:, :], 0.0).then_inc(made, 1)
                dve.wait_ge(loaded, 16 * (11 + 2 * B))
                dve.wait_ge(made, 2)
                for half in range(2):
                    r = 64 * half
                    nc.vector.tensor_copy(sel_o[r:r + D, :], id_sb[r:r + D, r:r + D])
                    nc.vector.memset(sel_d[r + D:r + D + 1, :], 1.0)
        clear(nc, names)

        q_proj, x_used, split_ready, split_stored, v_ready, psum_read = [
            sem(n) for n in ("q_proj", "x_used", "split_ready", "split_stored", "v_ready", "psum_read")]
        f_ready = sem("f_ready")
        x_even, x_odd, st_even, st_odd = sem("x_even"), sem("x_odd"), sem("st_even"), sem("st_odd")

        def project(b):
            with nc.Block() as block:
                xc = exps[:, 0, :].rearrange("p (a b) -> p a b", a=2)
                full = lambda r, i: work(2 + 2 * r + i)
                hilo = lambda r, i, part: q_dst[:, r, i, part, :]
                q_dst = split_buf

                @block.sync
                def _(sp):
                    sp.sem_inc(x_used, 2)
                    sp.sem_inc(st_even, 16 * 4)
                    sp.sem_inc(st_odd, 16 * 4)
                    with sp.Fori(0, NCH // 2) as k:
                        for r in range(2):
                            sp.wait_ge(x_used, k * 2 + r + 1)
                            sp.dma_start(xc[:, r, :], x[b, :, bass.ts(k * 2 + r, CH)]).then_inc((x_even, x_odd)[r], 16)

                @block.tensor
                def _(pe):
                    with pe.Fori(0, NCH // 2) as k:
                        for r in range(2):
                            c = k * 2 + r
                            pe.wait_ge((x_even, x_odd)[r], 16 * k + 16)
                            pe.wait_ge(psum_read, c + 1)
                            pe.wait_ge(v_ready, c + 1)
                            for i in range(2):
                                nc.tensor.matmul(ps[:, 3 * r + i, :], w_sb[:, i, :], xc[:, r, :],
                                                 start=True, stop=True).then_inc(q_proj, 1)
                            for j in range(CH // 128):
                                last = nc.tensor.matmul(ps[:, 3 * r + 2, 128 * j:128 * j + 128],
                                                        xc[:, r, 128 * j:128 * j + 128], w_sb[:, 2, :],
                                                        start=True, stop=True)
                            last.then_inc(x_used, 1)

                @block.scalar
                def _(act):
                    act.sem_inc(psum_read, 2)
                    with act.Fori(0, NCH // 2) as k:
                        for r in range(2):
                            c = k * 2 + r
                            act.wait_ge(split_ready, c + 1)
                            for i in range(2):
                                act.wait_ge(q_proj, c * 2 + i + 1)
                                ins = nc.scalar.activation(full(r, i), ps[:, 3 * r + i, :], ACT.Identity,
                                                           bias=bias[:, i:i + 1])
                                if i == 0:
                                    ins.then_inc(f_ready, 1)
                            ins.then_inc(psum_read, 1)
                            act.wait_ge(split_ready, c + 3)
                            for i in range(2):
                                for part in range(2):
                                    act.dma_start(qk_split[i, part, :, bass.ts(c, CH)], hilo(r, i, part).bitcast(F32)
                                                  ).then_inc((st_even, st_odd)[r], 16)

                @block.vector
                def _(dve):
                    dve.sem_inc(split_ready, 2)
                    dve.sem_inc(v_ready, 2)
                    with dve.Fori(0, NCH // 2) as k:
                        for r in range(2):
                            c = k * 2 + r
                            dve.wait_ge(x_used, c + 3)
                            vt = v_next[:, :, bass.ts(c, CH // 128), 0:D].rearrange("p h t d -> p t h d")
                            nc.vector.tensor_tensor(
                                vt, ps[:, 3 * r + 2, :].rearrange("p (t h d) -> p t h d", t=CH // 128, d=D),
                                bv_sb[:, :].rearrange("p (o h d) -> p o h d", o=1, d=D).to_broadcast([128, CH // 128, HEADS, D]),
                                ALU.add).then_inc(v_ready, 1)
                            dve.wait_ge((st_even, st_odd)[r], 64 * k + 64)
                            dve.wait_ge(psum_read, c + 3)
                            for i in range(2):
                                nc.vector.tensor_copy(hilo(r, i, 0), full(r, i)).then_inc(made, 1)
                            for i in range(2):
                                dve.wait_ge(made, c * 2 + i + 1)
                                last = nc.vector.tensor_tensor(hilo(r, i, 1), full(r, i), hilo(r, i, 0).bitcast(F32), ALU.subtract)
                            last.then_inc(split_ready, 1)

                @block.gpsimd
                def _(pool):
                    pool.wait_ge(st_even, 64 * (NCH // 2) + 64)
                    pool.wait_ge(st_odd, 64 * (NCH // 2) + 64)
            clear(nc, names)

        k_first, k_rest = sem("k_first"), sem("k_rest")
        q_piece = [sem(f"q_piece{i}") for i in range(NCH)]
        smax_ready, smax_done, sexp_ready, exp_done, av_done, out_read = [
            sem(n) for n in ("smax_ready", "smax_done", "sexp_ready", "exp_done", "av_done", "out_read")]
        mneg_ready, mt_ready, mrow_hi, mrow_ready, mrow_stored = [
            sem(n) for n in ("mneg_ready", "mt_ready", "mrow_hi", "mrow_ready", "mrow_stored")]

        def attend(h, nxt):
            buf, nbuf = (h or 0) % 2 if h is not None else None, nxt % 2 if nxt is not None else None

            def over_chunks(e, part, lead=None):
                if lead:
                    lead()
                with e.Fori(0, NCH // 2 - 1) as k:
                    for r in range(2):
                        part(k * 2 + r, r)
                for r in range(2):
                    part(NCH - 2 + r, r)

            with nc.Block() as block:
                @block.sync
                def _(sp):
                    if nxt is not None:
                        hd = slice(D * nxt, D * nxt + D)

                        def rows(i, c0, c1, sem_):
                            for n, part in enumerate(((0, 1, 0), (0, 0, 1))[i]):
                                sp.dma_start((q_st, k_st)[i][D * n:D * n + D, nbuf, c0 * CH:c1 * CH].bitcast(F32),
                                             qk_split[i, part, hd, c0 * CH:c1 * CH]).then_inc(sem_, 16)
                        rows(1, 0, 1, k_first)
                        rows(0, 0, 1, q_piece[0])
                        rows(0, 1, 2, q_piece[1])
                        rows(1, 1, NCH, k_rest)
                        for c in range(2, NCH):
                            rows(0, c, c + 1, q_piece[c])
                        sp.wait_ge(mrow_ready, 1)
                        for part in range(2):
                            sp.dma_start(q_st[PARTS + part:PARTS + part + 1, nbuf, :].bitcast(F32), mrow[:, part, :].bitcast(F32)).then_inc(mrow_stored, 16)
                        sp.wait_ge(mrow_stored, 32)

                @block.tensor
                def _(pe):
                    def max_tile(c, r, t):
                        if t % (CH // 128) == 0:
                            pe.wait_ge(q_piece[t // (CH // 128)], 48)
                        if t == 0:
                            pe.wait_ge(k_rest if r else k_first, 48)
                        pe.wait_ge(smax_done, c * NT + t + 1)
                        nc.tensor.matmul(ps[:, t % 2, :], q_st[0:PARTS, nbuf, 128 * t:128 * t + 128],
                                         k_st[0:PARTS, nbuf, bass.ts(c, CH)], start=True, stop=True).then_inc(smax_ready, 1)

                    def exp_tile(c, u, i):
                        t = 2 * u + i
                        if i == 0:
                            pe.wait_ge(exp_done, c * PAIRS + u + 1)
                        ins = nc.tensor.matmul(ps[:, 2 + 2 * (u % 2) + i, :], k_st[0:SHIFT, buf, 128 * t:128 * t + 128],
                                               q_st[0:SHIFT, buf, bass.ts(c, CH)], start=True, stop=True)
                        if i:
                            ins.then_inc(sexp_ready, 1)

                    def scores(c, r, u):
                        for i in range(2):
                            if nxt is not None:
                                max_tile(c, r, 2 * u + i)
                            if h is not None:
                                exp_tile(c, u, i)

                    def attn_v(c, r, u):
                        if u == 0:
                            pe.wait_ge(out_read, c + 1)
                        pe.wait_ge(exp_done, c * PAIRS + u + 3)
                        for i in range(2):
                            t = 2 * u + i
                            ins = nc.tensor.matmul(ps[64 * i:64 * i + D + 1, 6 + r, :], v_cur[:, h, t, :],
                                                   exps[:, u % 4, CH * i:CH * i + CH], start=(u == 0), stop=(u == PAIRS - 1))
                        ins.then_inc(av_done, 1)

                    AHEAD = 2

                    def part(c, r):
                        for u in range(PAIRS):
                            if u + AHEAD < PAIRS:
                                scores(c, r, u + AHEAD)
                            elif not isinstance(c, int) or c + 1 < NCH:
                                scores(c + 1, 1 - r, u + AHEAD - PAIRS)
                            if h is not None:
                                attn_v(c, r, u)

                    over_chunks(pe, part, lambda: [scores(0, 0, u) for u in range(AHEAD)])
                    if nxt is not None:
                        pe.wait_ge(mneg_ready, 1)
                        nc.tensor.transpose(ps[0:NT, 0, 0:128], mneg[:, :], id_sb[:, :]).then_inc(mt_ready, 1)

                @block.scalar
                def _(act):
                    if h is None:
                        return
                    act.sem_inc(exp_done, 2)
                    act.sem_inc(out_read, 2)

                    def read_out(c, r):
                        act.wait_ge(av_done, c * PAIRS + PAIRS + 4)
                        nc.scalar.copy(heads_out[:, h, bass.ts(c, CH)], ps[:, 6 + r, :]).then_inc(out_read, 1)

                    def part(c, r):
                        for u in range(PAIRS):
                            n = c * PAIRS + u
                            act.wait_ge(sexp_ready, n + 1)
                            act.wait_ge(av_done, n + 1)
                            nc.scalar.activation(exps[:, u % 4, :], ps[:, 2 + 2 * (u % 2):4 + 2 * (u % 2), :].rearrange("p a b -> p (a b)"),
                                                 ACT.Exp, scale=SCALE).then_inc(exp_done, 1)
                            if u == 3 and (not isinstance(c, int) or c > 0):
                                read_out(c - 1, 1 - r)

                    part(0, 0)
                    with act.Fori(0, NCH // 2 - 1) as k:
                        for r in range(2):
                            part(k * 2 + r + 1, 1 - r)
                    part(NCH - 1, 1)
                    read_out(NCH - 1, 1)

                @block.gpsimd
                def _(pool):
                    if h is not None:
                        pool.sem_inc(av_done, 4)

                @block.vector
                def _(dve):
                    if nxt is None:
                        return
                    dve.sem_inc(smax_done, 2)
                    with dve.Fori(0, NCH) as c:
                        for t in range(NT):
                            dve.wait_ge(smax_ready, c * NT + t + 1)
                            nc.vector.tensor_reduce(mpart[:, c, t:t + 1], ps[:, t % 2, :], AX.X, ALU.max).then_inc(smax_done, 1)
                    dve.wait_ge(smax_done, NCH * NT + 2)
                    nc.vector.tensor_reduce(mneg[:, :], mpart[:, :, :].rearrange("p c t -> p t c"), AX.X, ALU.max,
                                            negate=True).then_inc(mneg_ready, 1)
                    dve.wait_ge(mt_ready, 1)
                    nc.vector.tensor_copy(mrow[:, 0, :], ps[0:NT, 0, 0:128]).then_inc(mrow_hi, 1)
                    dve.wait_ge(mrow_hi, 1)
                    nc.vector.tensor_tensor(mrow[:, 1, :], ps[0:NT, 0, 0:128], mrow[:, 0, :].bitcast(F32), ALU.subtract).then_inc(mrow_ready, 1)
            clear(nc, names)

        def take_v():
            with nc.Block() as block:
                @block.vector
                def _(dve):
                    nc.vector.tensor_copy(v_cur[:, :, :, :], v_next[:, :, :, :])

        (od_ready, log_d, recip_d, normed, wo_ready, y_ready, mean_ready, centred, squared, var_ready, log_v, rstd_ready,
         scaled, z_ready, flipped, z_stored) = [sem(n) for n in (
             "od_ready", "log_d", "recip_d", "normed", "wo_ready", "y_ready", "mean_ready", "centred", "squared", "var_ready", "log_v",
             "rstd_ready", "scaled", "z_ready", "flipped", "z_stored")]

        def finish(b):
            X_IN, RECIP, NORMED, Y, CENTRED, SQUARE, RSTD = range(7)
            buf = lambda what, r: work(2 * what + r)
            Z, SCALED, FLIP = range(3)
            with nc.Block() as block:
                @block.sync
                def _(sp):
                    sp.sem_inc(y_ready, 2)
                    with sp.Fori(0, NCH // 2) as k:
                        for r in range(2):
                            c = k * 2 + r
                            sp.wait_ge(y_ready, c + 1)
                            sp.dma_start(buf(X_IN, r), x[b, :, bass.ts(c, CH)]).then_inc((x_even, x_odd)[r], 16)
                    sp.wait_ge(z_ready, NCH)
                    sp.dma_start(z_ext[b, :, W:W + L], heads_out[:, Z, :]).then_inc(z_stored, 16)
                    sp.wait_ge(flipped, 4)
                    sp.dma_start(z_flip[b, :, :], heads_out[:, FLIP, :]).then_inc(z_stored, 16)
                    sp.wait_ge(z_stored, 32)

                @block.gpsimd
                def _(pool):
                    pool.wait_ge(z_ready, NCH)
                    z = heads_out[:, Z, :].rearrange("p (h w) -> p h w", w=W)
                    f = heads_out[:, FLIP, :].rearrange("p (h w) -> p h w", w=W)
                    for fh, zh in ((slice(0, 1), slice(0, 1)), (slice(1, H), slice(H - 1, 0, -1))):
                        for fw, zw in ((slice(0, 1), slice(0, 1)), (slice(1, W), slice(W - 1, 0, -1))):
                            pool.tensor_copy(f[:, fh, fw], z[:, zh, zw]).then_inc(flipped, 1)

                @block.tensor
                def _(pe):
                    for step in range(NCH + 3):
                        c = step
                        if c < NCH:
                            pe.wait_ge(normed, c + 1)
                            for sel, bank in ((sel_o, 0), (sel_d, 1)):
                                for h in range(HEADS):
                                    ins = nc.tensor.matmul(ps[D * h:D * h + D, bank, :], sel[:, :],
                                                           heads_out[:, h, c * CH:c * CH + CH], start=True, stop=True)
                            ins.then_inc(od_ready, 1)
                        c, r = step - 1, (step - 1) % 2
                        if 0 <= c < NCH:
                            pe.wait_ge(normed, c + 2)
                            pe.wait_ge(y_ready, c + 1)
                            nc.tensor.matmul(ps[:, 2 + r, :], w_sb[:, 3, :], buf(NORMED, r), start=True, stop=True).then_inc(wo_ready, 1)
                        c, r = step - 2, step % 2
                        if 0 <= c < NCH:
                            pe.wait_ge(y_ready, c + 3)
                            pe.wait_ge(centred, c + 1)
                            nc.tensor.matmul(ps[:, 4 + r, :], ones_c[:, :], buf(Y, r), start=True, stop=True).then_inc(mean_ready, 1)
                        c, r = step - 3, (step - 3) % 2
                        if 0 <= c < NCH:
                            pe.wait_ge(squared, c + 1)
                            pe.wait_ge(rstd_ready, c + 1)
                            nc.tensor.matmul(ps[:, 6 + r, :], ones_c[:, :], buf(SQUARE, r), start=True, stop=True).then_inc(var_ready, 1)

                @block.scalar
                def _(act):
                    act.sem_inc(rstd_ready, 2)

                    def emit(step, par, stages):
                        if 0 in stages:
                            c, r = step, par
                            act.wait_ge(od_ready, c + 1)
                            act.wait_ge(normed, c + 1)
                            nc.scalar.activation(buf(RECIP, r), ps[:, 1, :], ACT.Ln).then_inc(log_d, 1)
                            act.wait_ge(log_d, c + 1)
                            nc.scalar.activation(buf(RECIP, r), buf(RECIP, r), ACT.Exp, scale=-1.0).then_inc(recip_d, 1)
                        if 2 in stages:
                            c, r = step - 2, par
                            act.wait_ge(centred, c + 3)
                            nc.scalar.activation(buf(SQUARE, r), buf(CENTRED, r), ACT.Square).then_inc(squared, 1)
                        if 3 in stages:
                            c, r = step - 3, (par - 3) % 2
                            act.wait_ge(var_ready, c + 1)
                            act.wait_ge(scaled, c + 1)
                            nc.scalar.activation(buf(RSTD, r), ps[:, 6 + r, :], ACT.Ln, bias=eps[:, 0:1]).then_inc(log_v, 1)
                            act.wait_ge(log_v, c + 1)
                            nc.scalar.activation(buf(RSTD, r), buf(RSTD, r), ACT.Exp, scale=-0.5).then_inc(rstd_ready, 1)
                        if 4 in stages:
                            c = step - 4
                            act.wait_ge(scaled, c + 3)
                            nc.scalar.activation(heads_out[:, Z, bass.ts(c, CH)], heads_out[:, SCALED, bass.ts(c, CH)], ACT.Identity,
                                                 bias=bias[:, 4:5], scale=bias[:, 3:4]).then_inc(z_ready, 1)
                    pipelined(act, NCH, 5, emit)

                @block.vector
                def _(dve):
                    dve.sem_inc(normed, 1)
                    dve.sem_inc(centred, 2)
                    dve.sem_inc(scaled, 2)

                    def emit(step, par, stages):
                        if 0 in stages:
                            c, r = step, par
                            dve.wait_ge(recip_d, c + 1)
                            nc.vector.tensor_tensor(buf(NORMED, r), ps[:, 0, :], buf(RECIP, r), ALU.mult).then_inc(normed, 1)
                        if 1 in stages:
                            c, r = step - 1, (par - 1) % 2
                            dve.wait_ge((x_even, x_odd)[r], (c - r) * 8 + 16)
                            dve.wait_ge(wo_ready, c + 1)
                            nc.vector.scalar_tensor_tensor(buf(Y, r), ps[:, 2 + r, :], bias[:, 2:3], buf(X_IN, r), ALU.add, ALU.add
                                                           ).then_inc(y_ready, 1)
                        if 2 in stages:
                            c, r = step - 2, par
                            dve.wait_ge(mean_ready, c + 1)
                            dve.wait_ge(scaled, c + 1)
                            nc.vector.tensor_tensor(buf(CENTRED, r), buf(Y, r), ps[:, 4 + r, :], ALU.subtract).then_inc(centred, 1)
                        if 3 in stages:
                            c, r = step - 3, (par - 3) % 2
                            dve.wait_ge(rstd_ready, c + 3)
                            nc.vector.tensor_tensor(heads_out[:, SCALED, bass.ts(c, CH)], buf(CENTRED, r), buf(RSTD, r), ALU.mult
                                                    ).then_inc(scaled, 1)
                    pipelined(dve, NCH, 4, emit)
            clear(nc, names)

        def batch(b, last):
            take_v()
            for h in range(HEADS):
                if h == HEADS - 1:
                    if not last:
                        project(b + 1)
                    attend(h, None if last else 0)
                else:
                    attend(h, h + 1)
            finish(b)

        project(0)
        attend(None, 0)
        if nb > 1:
            with nc.Fori(0, nb - 1) as b:
                batch(b, False)
        batch(nb - 1, True)


ST = 16
GC = 128 // ST
INNER = 2 * C
LC = 1024
STEPS = L // LC
ROWS = LC // W
HALO = (ROWS + 2) * W
GROUPS = INNER // GC
RANK = 8


def layer1(nc, z_ext, z_flip, w, out, nb=B):
    with ExitStack() as ctx:
        def sb(name, shape, dt=F32):
            return ctx.enter_context(nc.sbuf_tensor(name, shape, dt))

        names = []

        def sem(name):
            s = ctx.enter_context(nc.semaphore(name))
            names.append(s)
            return s

        ps = ctx.enter_context(nc.psum_tensor("ps1", [128, 8, CH], F32))
        win = sb("win", [C, 2 * INNER])
        wtap = sb("wtap", [C, 4, INNER])
        taps_bc = sb("taps_bc", [C, 4, INNER])
        wxd = sb("wxd", [128, 2, 128])
        wdt = sb("wdt", [128, INNER])
        sel_b = sb("sel_b", [128, 128])
        sel_c = sb("sel_c", [128, 128])
        sel_g = sb("sel_g", [128, 8, 128], F32R)
        sel_y = sb("sel_y", [128, 4, 32])
        wconv = sb("wconv", [C, 9, C])
        wspec = sb("wspec", [C, 4, C])
        wmix = sb("wmix", [C, 4, C])
        hilb = sb("hilb", [128, 128])
        wout = sb("wout", [128, 2, C])
        cols = sb("cols", [128, 9])
        a_neg = sb("a_neg", [128, GROUPS])
        carry = sb("carry", [128, GROUPS])
        row0 = sb("row0", [128, STEPS, W])
        hil0 = sb("hil0", [128, W])
        stage_z = sb("stage_z", [128, HALO])
        stage_j = sb("stage_j", [128, LC])
        za = sb("za", [128, HALO])
        zp = sb("zp", [128, ROWS + 2, W + 2])
        zj = sb("zj", [128, LC])
        xs = sb("xs", [128, 2, LC])
        gz = sb("gz", [128, 2, LC])
        vdt = sb("vdt", [128, 2, LC])
        edt = sb("edt", [128, 2, LC])
        dt = sb("dt", [128, 2, LC])
        ux = edt
        xd = sb("xd", [128, LC])
        s_dt = sb("s_dt", [128, 4, LC], F32R)
        s_u = sb("s_u", [128, 4, LC], F32R)
        b_rep = sb("b_rep", [128, LC])
        c_rep = sb("c_rep", [128, LC])
        g_t = sb("g_t", [128, LC])
        NDA, NBU, NHH, NHC = 3, 2, 3, 6
        d_a = sb("d_a", [128, NDA, LC])
        b_u = sb("b_u", [128, NBU, LC])
        hh = sb("hh", [128, NHH, LC])
        hc = sb("hc", [128, NHC, LC])
        yt = vdt
        o_sb = d_a[:, 0, :]

        loaded, made, made2, a_exp = sem("loaded1"), sem("made1"), sem("made2"), sem("a_exp")
        with nc.Block() as block:
            @block.sync
            def _(sp):
                n = [0]

                def load(dst, src):
                    sp.dma_start(dst, src).then_inc(loaded, 16)
                    n[0] += 16
                load(win[:, :], w["win"])
                load(taps_bc[:, :, :], w["taps"].rearrange("(o k) e -> o k e", o=1).to_broadcast([C, 4, INNER]))
                load(wxd[:, :, :], w["wxd"])
                load(wdt[:, :], w["wdt"])
                load(sel_b[:, :], w["sel_b"])
                load(sel_c[:, :], w["sel_c"])
                load(hh[:, 0, :], w["sel_g"])
                load(sel_y[:, :, :], w["sel_y"])
                load(wconv[:, :, :], w["wconv"])
                load(wspec[:, :, :], w["wspec"])
                load(hilb[:, :], w["hilb"])
                load(hil0[:, :], w["hil0"].to_broadcast([128, W]))
                load(wout[:, :, :], w["wout"])
                load(cols[:, :], w["cols"])
                load(a_neg[:, :], w["a_log"])
                sp.wait_ge(loaded, n[0])
            NLOAD = 15 * 16

            @block.gpsimd
            def _(pool):
                pool.memset(zp[:, :, :], 0.0)
                pool.memset(row0[:, :, :], 0.0).then_inc(made, 1)

            @block.scalar
            def _(act):
                act.wait_ge(loaded, NLOAD)
                nc.scalar.activation(a_neg[:, :], a_neg[:, :], ACT.Exp).then_inc(a_exp, 1)
                act.wait_ge(a_exp, 1)
                nc.scalar.mul(a_neg[:, :], a_neg[:, :], -1.0)

            @block.vector
            def _(dve):
                dve.wait_ge(loaded, NLOAD)
                nc.vector.tensor_copy(sel_g[:, :, :].rearrange("p a b -> p (a b)"), hh[:, 0, :])
                nc.vector.tensor_tensor(wtap[:, :, :], taps_bc[:, :, :],
                                        win[:, 0:INNER].rearrange("p (o e) -> p o e", o=1).to_broadcast([C, 4, INNER]), ALU.mult)
                RR, RI, IR, II = range(4)
                nc.vector.tensor_tensor(wmix[:, 0, :], wspec[:, RR, :], wspec[:, II, :], ALU.add)
                nc.vector.tensor_tensor(wmix[:, 1, :], wspec[:, RR, :], wspec[:, II, :], ALU.subtract)
                nc.vector.tensor_tensor(wmix[:, 2, :], wspec[:, IR, :], wspec[:, RI, :], ALU.subtract)
                nc.vector.tensor_tensor(wmix[:, 3, :], wspec[:, IR, :], wspec[:, RI, :], ALU.add).then_inc(made2, 1)
                dve.wait_ge(made2, 1)
                dve.wait_ge(made, 1)
                nc.vector.tensor_scalar_mul(wmix[:, :, :], wmix[:, :, :], 0.5).then_inc(made, 1)
                nc.vector.tensor_scalar(row0[:, 0, :], hil0[:, :], cols[:, 8:9], None, ALU.mult).then_inc(made, 1)
                dve.wait_ge(made, 3)
                nc.vector.tensor_tensor(wconv[:, 4, :], wconv[:, 4, :], wmix[:, 0, :], ALU.add)
                nc.vector.tensor_tensor(row0[:, 0, 0:1], row0[:, 0, 0:1], cols[:, 7:8], ALU.add)
        clear(nc, names)

        (z_in, z_copied, item, item_read, xs_ready, sp_pos, sp_log, dt_ready, u_ready, hi_ready, lo_ready,
         dt_rep, u_rep, da_ready, bu_ready, scanned, carried, hc_ready, y_done, y_read, t_ready, gated, o_ready, o_copied, o_full, o_stored,
         v_ready, prefetched) = [sem(x) for x in (
             "z_in", "z_copied", "item", "item_read", "xs_ready", "sp_pos", "sp_log", "dt_ready1", "u_ready", "hi_ready", "lo_ready",
             "dt_rep", "u_rep", "da_ready", "bu_ready", "scanned", "carried", "hc_ready", "y_done", "y_read", "t_ready", "gated", "o_ready",
             "o_copied", "o_full", "o_stored", "v_ready1", "prefetched")]

        items = ([("xs", h, q) for h in range(2) for q in range(2)] + [("gate", 0, 0), ("gate", 0, 1)]
                 + [("xd", 0, q) for q in range(2)] + [("gate", 1, 0), ("gate", 1, 1)]
                 + [("dt", h, q) for h in range(2) for q in range(2)]
                 + [(x, 0, q) for x in ("b", "c") for q in range(2)] + [("g", 0, q) for q in range(2)])
        NI = len(items)
        at = {x: n for n, x in enumerate(items)}
        RING = 6

        def step(b, lc):
            with nc.Block() as block:
                @block.sync
                def _(sp):
                    sp.dma_start(stage_z[:, :], z_ext[b, :, bass.ds(lc * LC, HALO)]).then_inc(z_in, 16)
                    sp.dma_start(stage_j[:, :], z_flip[b, :, bass.ts(lc, LC)]).then_inc(z_in, 16)
                    sp.wait_ge(o_full, 1)
                    sp.dma_start(out[b, :, bass.ts(lc, LC)], o_sb).then_inc(o_stored, 16)
                    sp.wait_ge(o_stored, 16)

                @block.tensor
                def _(pe):
                    pe.wait_ge(z_copied, 3)
                    for n, (what, h, q) in enumerate(items):
                        bank = ps[:, n % RING, :]
                        if n >= RING:
                            pe.wait_ge(item_read, n - RING + 1)
                        qs = slice(q * CH, q * CH + CH)
                        hs = slice(h * 128, h * 128 + 128)
                        if what == "xs":
                            for k in range(4):
                                ins = nc.tensor.matmul(bank, wtap[:, k, hs], za[:, W - 3 + k + q * CH:W - 3 + k + q * CH + CH],
                                                       start=(k == 0), stop=(k == 3))
                        elif what == "gate":
                            ins = nc.tensor.matmul(bank, win[:, INNER + h * 128:INNER + h * 128 + 128], za[:, W + q * CH:W + q * CH + CH],
                                                   start=True, stop=True)
                        elif what == "xd":
                            pe.wait_ge(item_read, at["xs", 1, q] + 1)
                            for i in range(2):
                                ins = nc.tensor.matmul(bank, wxd[:, i, :], xs[:, i, qs], start=(i == 0), stop=(i == 1))
                        elif what == "g":
                            for j in range(4):
                                p0 = q * CH + j * 128
                                nc.tensor.matmul(bank[:, j * 128:j * 128 + 128], za[:, W + p0:W + p0 + 128], wmix[:, 2, :],
                                                 start=True, stop=False)
                                ins = nc.tensor.matmul(bank[:, j * 128:j * 128 + 128], zj[:, p0:p0 + 128], wmix[:, 3, :],
                                                       start=False, stop=True)
                        else:
                            pe.wait_ge(item_read, at["xd", 0, q] + 1)
                            lhs = {"dt": wdt[:, hs], "b": sel_b[:, :], "c": sel_c[:, :]}[what]
                            ins = nc.tensor.matmul(bank, lhs, xd[:, qs], start=True, stop=True)
                        ins.then_inc(item, 1)

                    extra = []
                    for q in range(2):
                        o = ps[:, 6 + q, :]
                        for k in range(9):
                            dy, dx = k // 3, k % 3
                            rhs = zp[:, q * 8 + dy:q * 8 + dy + 8, dx:dx + W]
                            extra.append((o.rearrange("p (a b) -> p a b", b=W), wconv[:, k, :], rhs, k == 0))
                        extra.append((o, wmix[:, 1, :], zj[:, q * CH:q * CH + CH], False))
                        for j in range(4):
                            p0 = q * CH + j * 128
                            extra.append((o[:, j * 128:j * 128 + 128], g_t[:, p0:p0 + 128], hilb[:, :], False))

                    def fill():
                        if extra:
                            o, lhs, rhs, first = extra.pop(0)
                            nc.tensor.matmul(o, lhs, rhs, start=first, stop=False)

                    def reduce_states(batch):
                        half, jj = batch // 4, batch % 4
                        pe.wait_ge(hc_ready, 4 * batch + 4)
                        if half == 1 and jj == 0:
                            pe.wait_ge(t_ready, 1)
                        for q in range(2):
                            for i in range(4):
                                ins = nc.tensor.matmul(ps[32 * i:32 * i + 32, 4 + q, :], sel_y[:, jj, :],
                                                       hc[:, (4 * batch + i) % NHC, q * CH:q * CH + CH],
                                                       start=(jj == 0), stop=(jj == 3))
                        ins.then_inc(y_done, 1)

                    pe.wait_ge(item_read, NI)
                    for g in range(GROUPS):
                        half, jj, i = g // 16, g // 4 % 4, g % 4
                        s, j = 2 * half + i // 2, jj + 4 * (i % 2)
                        if g == 0:
                            pe.wait_ge(lo_ready, 2)
                        else:
                            pe.wait_ge(da_ready, g)
                        for q in range(2):
                            ins = nc.tensor.matmul(ps[:, q, :], sel_g[:, j, :], s_dt[:, s, q * CH:q * CH + CH], start=True, stop=True)
                        ins.then_inc(dt_rep, 1)
                        if g == 0:
                            pe.wait_ge(lo_ready, 4)
                        else:
                            pe.wait_ge(bu_ready, g)
                        for q in range(2):
                            ins = nc.tensor.matmul(ps[:, 2 + q, :], sel_g[:, j, :], s_u[:, s, q * CH:q * CH + CH], start=True, stop=True)
                        ins.then_inc(u_rep, 1)
                        fill()
                        if g >= 5 and g % 4 == 1:
                            reduce_states(g // 4 - 1)
                    reduce_states(GROUPS // 4 - 1)
                    while extra:
                        fill()
                    pe.wait_ge(gated, 2)
                    for q in range(2):
                        for i in range(2):
                            ins = nc.tensor.matmul(ps[:, 6 + q, :], wout[:, i, :], yt[:, i, q * CH:q * CH + CH], start=False, stop=(i == 1))
                    ins.then_inc(o_ready, 1)

                @block.scalar
                def _(act):
                    act.wait_ge(z_in, 32)
                    nc.scalar.copy(zp[:, :, 1:W + 1], stage_z[:, :].rearrange("p (a b) -> p a b", b=W)).then_inc(z_copied, 1)
                    for n, (what, h, q) in enumerate(items):
                        bank = ps[:, n % RING, :]
                        qs = slice(q * CH, q * CH + CH)
                        act.wait_ge(item, n + 1)
                        if what == "xs":
                            ins = nc.scalar.activation(xs[:, h, qs], bank, ACT.Silu, bias=cols[:, h:h + 1])
                        elif what == "gate":
                            ins = nc.scalar.activation(gz[:, h, qs], bank, ACT.Silu)
                        elif what == "dt":
                            ins = nc.scalar.activation(vdt[:, h, qs], bank, ACT.Identity, bias=cols[:, 2 + h:3 + h])
                        else:
                            ins = nc.scalar.copy({"xd": xd, "b": b_rep, "c": c_rep, "g": g_t}[what][:, qs], bank)
                        ins.then_inc(item_read, 1)
                        if what == "dt" and h == 1 and q == 1:
                            act.wait_ge(item_read, n + 1)
                            nc.scalar.activation(edt[:, :, :], vdt[:, :, :], ACT.Abs).then_inc(sp_log, 1)
                            act.wait_ge(sp_log, 1)
                            nc.scalar.activation(edt[:, :, :], edt[:, :, :], ACT.Exp, scale=-1.0).then_inc(sp_log, 1)
                            act.wait_ge(sp_log, 2)
                            nc.scalar.activation(edt[:, :, :], edt[:, :, :], ACT.Ln, bias=1.0).then_inc(sp_log, 1)

                    def keep(g):
                        act.wait_ge(scanned, g + 1)
                        half, jj, i = g // 16, g // 4 % 4, g % 4
                        col = (2 * half + i // 2) * 8 + jj + 4 * (i % 2)
                        nc.scalar.copy(carry[:, col:col + 1], hh[:, g % NHH, LC - 1:LC]).then_inc(carried, 1)

                    for g in range(GROUPS):
                        half, jj, i = g // 16, g // 4 % 4, g % 4
                        col = (2 * half + i // 2) * 8 + jj + 4 * (i % 2)
                        act.wait_ge(dt_rep, g + 1)
                        if g >= NDA:
                            act.wait_ge(scanned, g - NDA + 1)
                        nc.scalar.activation(d_a[:, g % NDA, :], ps[:, 0:2, :].rearrange("p a b -> p (a b)"), ACT.Exp,
                                             scale=a_neg[:, col:col + 1]).then_inc(da_ready, 1)
                        if g >= 2:
                            keep(g - 2)
                    keep(GROUPS - 2)
                    keep(GROUPS - 1)
                    act.wait_ge(o_ready, 1)
                    nc.scalar.activation(o_sb, ps[:, 6:8, :].rearrange("p a b -> p (a b)"), ACT.Identity, bias=cols[:, 6:7]).then_inc(o_copied, 1)

                @block.vector
                def _(dve):
                    dve.wait_ge(z_in, 32)
                    nc.vector.tensor_copy(za[:, :], stage_z[:, :]).then_inc(z_copied, 1)
                    nc.vector.tensor_copy(zj[:, :], stage_j[:, :]).then_inc(z_copied, 1)
                    dve.wait_ge(item_read, at["dt", 1, 1] + 1)
                    nc.vector.tensor_scalar_max(dt[:, :, :], vdt[:, :, :], 0.0).then_inc(sp_pos, 1)
                    dve.wait_ge(sp_pos, 1)
                    dve.wait_ge(sp_log, 3)
                    nc.vector.tensor_tensor(dt[:, :, :], dt[:, :, :], edt[:, :, :], ALU.add).then_inc(dt_ready, 1)
                    dve.wait_ge(dt_ready, 1)
                    for n, (stack, src) in enumerate(((s_dt, dt), (s_u, ux))):
                        if n == 1:
                            nc.vector.tensor_tensor(ux[:, :, :], dt[:, :, :], xs[:, :, :], ALU.mult).then_inc(u_ready, 1)
                            dve.wait_ge(u_ready, 1)
                        for part in range(2):
                            p = slice(64 * part, 64 * part + 64)
                            nc.vector.tensor_copy(stack[p, part::2, :], src[p, :, :]).then_inc(hi_ready, 1)
                        for part in range(2):
                            p, r = slice(64 * part, 64 * part + 64), slice(64 - 64 * part, 128 - 64 * part)
                            dve.wait_ge(hi_ready, 2 * n + part + 1)
                            nc.vector.tensor_tensor(stack[r, part::2, :], src[p, :, :], stack[p, part::2, :].bitcast(F32), ALU.subtract
                                                    ).then_inc(lo_ready, 1)
                    dve.wait_ge(item_read, at["b", 0, 1] + 1)

                    def gate_y(half):
                        dve.wait_ge(y_done, 4 * half + 4)
                        nc.vector.scalar_tensor_tensor(yt[:, half, :], xs[:, half, :], cols[:, 4 + half:5 + half],
                                                       ps[:, 4:6, :].rearrange("p a b -> p (a b)"), ALU.mult, ALU.add).then_inc(t_ready, 1)
                        dve.wait_ge(t_ready, half + 1)
                        nc.vector.tensor_tensor(yt[:, half, :], yt[:, half, :], gz[:, half, :], ALU.mult).then_inc(gated, 1)

                    for g in range(GROUPS):
                        half, jj, i = g // 16, g // 4 % 4, g % 4
                        col = (2 * half + i // 2) * 8 + jj + 4 * (i % 2)
                        dve.wait_ge(u_rep, g + 1)
                        nc.vector.tensor_tensor(b_u[:, g % NBU, :], ps[:, 2:4, :].rearrange("p a b -> p (a b)"), b_rep[:, :], ALU.mult
                                                ).then_inc(bu_ready, 1)
                        dve.wait_ge(bu_ready, g + 1)
                        dve.wait_ge(da_ready, g + 1)
                        if g >= NHH:
                            dve.wait_ge(hc_ready, g - NHH + 1)
                            dve.wait_ge(carried, g - NHH + 1)
                        nc.vector.tensor_tensor_scan(hh[:, g % NHH, :], d_a[:, g % NDA, :], b_u[:, g % NBU, :], carry[:, col:col + 1],
                                                     ALU.mult, ALU.add).then_inc(scanned, 1)
                        if g == 18:
                            gate_y(0)
                    gate_y(1)
                    dve.wait_ge(o_copied, 1)
                    nc.vector.tensor_tensor(o_sb[:, 0:W], o_sb[:, 0:W], row0[:, lc, :], ALU.add).then_inc(o_full, 1)

                @block.gpsimd
                def _(pool):
                    pool.wait_ge(item_read, at["c", 0, 1] + 1)
                    for g in range(GROUPS):
                        pool.wait_ge(scanned, g + 1)
                        if g >= NHC:
                            pool.wait_ge(y_done, (g - NHC) // 4 + 1)
                        nc.gpsimd.tensor_tensor(hc[:, g % NHC, :], hh[:, g % NHH, :], c_rep[:, :], ALU.mult).then_inc(hc_ready, 1)
            clear(nc, names)

        with nc.Fori(0, nb) as b:
            with nc.Block() as block:
                @block.vector
                def _(dve):
                    nc.vector.memset(carry[:, :], 0.0)
            with nc.Fori(0, STEPS) as lc:
                step(b, lc)


def hilbert():
    s = np.zeros(W)
    s[1:W // 2], s[W // 2 + 1:] = 1, -1
    return np.real(np.fft.ifft(1j * s[:, None] * np.fft.fft(np.eye(W), axis=0), axis=0))


def host(i):
    f = np.float32
    c = np.ascontiguousarray
    w = {}
    w["win"] = c(i["L1_conv_in_proj_w"].T)
    w["taps"] = c(i["L1_conv_conv1d_w"][:, 0, :].T)
    xp = i["L1_conv_x_proj_w"]
    wx = np.zeros((128, 2, 128), f)
    wx[:, :, :40] = xp.reshape(40, 2, 128).transpose(2, 1, 0)
    w["wxd"] = wx
    wd = np.zeros((128, INNER), f)
    wd[:RANK] = i["L1_conv_dt_proj_w"].T
    w["wdt"] = wd
    p = np.arange(128)
    for name, off in (("sel_b", RANK), ("sel_c", RANK + ST)):
        m = np.zeros((128, 128), f)
        m[off + p % ST, p] = 1
        w[name] = m
    m = np.zeros((128, 8, 128), f)
    for j in range(8):
        for h in range(2):
            m[64 * h + 8 * j + p // ST, j, p] = 1
    w["sel_g"] = m.reshape(128, 1024)
    m = np.zeros((128, 4, 32), f)
    for j in range(4):
        m[p, j, 8 * j + p // ST] = 1
    w["sel_y"] = m
    w["wconv"] = c(i["L1_conv_conv_spatial_w"].reshape(C, C, 9).transpose(1, 2, 0))
    s = i["L1_conv_conv_spectral_w"][:, :, 0, 0].T
    w["wspec"] = c(np.stack([s[:C, :C], s[C:, :C], s[:C, C:], s[C:, C:]], 1))
    hm = hilbert()
    w["hilb"] = np.kron(np.eye(2), hm.T).astype(f)
    w["hil0"] = c(hm[:, 0][None]).astype(f)
    w["wout"] = c(i["L1_conv_out_proj_w"].reshape(C, 2, 128).transpose(2, 1, 0))
    two = lambda v: v.reshape(2, 128).T
    w["cols"] = c(np.concatenate([two(i["L1_conv_conv1d_b"]), two(i["L1_conv_dt_proj_b"]), two(i["L1_conv_D"]),
                                  i["L1_conv_conv_spatial_b"][:, None], two(i["L1_conv_conv_spectral_b"])], 1))
    w["a_log"] = c(i["L1_conv_A_log"].reshape(GROUPS, 128).T)
    return w


def build(nc, x, l0, w, out):
    z_ext = nc.dram_tensor("z_ext", [B, C, L + 2 * W], F32, kind="Internal").ap()
    z_flip = nc.dram_tensor("z_flip", [B, C, L], F32, kind="Internal").ap()
    layer0(nc, x, l0, z_ext, z_flip)
    layer1(nc, z_ext, z_flip, w, out)


def kernel(**inputs):
    import concourse.bacc as bacc
    from concourse.bass_utils import run_bass_kernel_spmd

    i = {k: np.asarray(v) for k, v in inputs.items()}
    l0 = {n: i["L0_conv_" + n] for n in ("Wq", "bq", "Wk", "bk", "Wv", "bv", "Wo", "bo", "gamma", "beta")}
    l0["ident"] = np.eye(128, dtype=np.float32)
    w = host(i)
    arrays = {"in_x": np.ascontiguousarray(i["x"].reshape(B, C, L))}
    arrays.update({"in_" + n: np.ascontiguousarray(v) for n, v in l0.items()})
    arrays.update({"in_" + n: np.ascontiguousarray(v) for n, v in w.items()})
    nc = bacc.Bacc("TRN2", target_bir_lowering=False, num_devices=1)
    aps = {n: nc.dram_tensor(n, v.shape, mybir.dt.from_np(v.dtype), kind="ExternalInput").ap() for n, v in arrays.items()}
    out = nc.dram_tensor("out", (B, C, L), F32, kind="ExternalOutput").ap()
    build(nc, aps["in_x"], {n: aps["in_" + n] for n in l0}, {n: aps["in_" + n] for n in w}, out)
    r = run_bass_kernel_spmd(nc, [arrays], core_ids=[0])
    return r.results[0]["out"].reshape(B, C, H, W)
```

```python
import numpy as np
import concourse.bass as bass
import concourse.mybir as mybir
from contextlib import ExitStack

F32, F32R = mybir.dt.float32, mybir.dt.float32r
ACT = mybir.ActivationFunctionType
ALU = mybir.AluOpType
AX = mybir.AxisListType

B, C, H, W = 4, 128, 64, 64
L = H * W
HEADS = 4
D = C // HEADS
SCALE = D ** -0.5
CH = 512
NCH = L // CH
NT = L // 128
PAIRS = NT // 2
LN_EPS = 1e-5
PARTS = 3 * D
SHIFT = PARTS + 2


def pipelined(e, n, depth, emit):
    lead = depth - 1 + (depth - 1) % 2
    for step in range(lead):
        emit(step, step % 2, [s for s in range(depth) if 0 <= step - s < n])
    with e.Fori(lead // 2, n // 2) as k:
        for r in range(2):
            emit(k * 2 + r, r, list(range(depth)))
    for step in range(n, n + depth - 1):
        emit(step, step % 2, [s for s in range(depth) if 0 <= step - s < n])


def clear(nc, sems):
    with nc.Block() as block:
        @block.vector
        def _(dve):
            for s in sems:
                dve.sem_clear(s)


def layer0(nc, x, w, z_ext, nb=B):
    qk_split = nc.dram_tensor("qk_split", [2, 2, C, L], F32, kind="Internal").ap()
    with ExitStack() as ctx:
        def sb(name, shape, dt=F32):
            return ctx.enter_context(nc.sbuf_tensor(name, shape, dt))

        names = []

        def sem(name):
            s = ctx.enter_context(nc.semaphore(name))
            names.append(s)
            return s

        ps = ctx.enter_context(nc.psum_tensor("ps", [128, 8, CH], F32))
        w_sb = sb("w_sb", [C, 4, C])
        bias = sb("bias", [C, 5])
        bv_sb = sb("bv_sb", [128, C])
        id_sb = sb("id_sb", [128, 128])
        ones_c = sb("ones_c", [C, C])
        sel_o = sb("sel_o", [128, D])
        sel_d = sb("sel_d", [128, D])
        eps = sb("eps", [128, 1])
        q_st = sb("q_st", [128, 2, L], F32R)
        k_st = sb("k_st", [128, 2, L], F32R)
        v_cur = sb("v_cur", [128, HEADS, NT, D + 1])
        v_next = sb("v_next", [128, HEADS, NT, D + 1])
        exps = sb("exps", [128, 4, 2 * CH])
        heads_out = sb("heads_out", [128, HEADS, L])
        mpart = sb("mpart", [128, NCH, NT])
        mneg = sb("mneg", [128, NT])
        mrow = sb("mrow", [NT, 2, 128], F32R)
        split_buf = sb("split_buf", [128, 2, 2, 2, CH], F32R)

        def work(i):
            if i < 8:
                return exps[:, i // 2, CH * (i % 2):CH * (i % 2) + CH]
            i -= 8
            return split_buf[:, i // 4, i // 2 % 2, i % 2, :].bitcast(F32)

        loaded = sem("loaded")
        made = sem("made")
        zero_ready = sem("zero_ready")

        with nc.Block() as block:
            @block.sync
            def _(sp):
                for i, name in enumerate(("Wq", "Wk", "Wv", "Wo")):
                    sp.dma_start(w_sb[:, i, :], w[name]).then_inc(loaded, 16)
                for i, name in enumerate(("bq", "bk", "bo", "gamma", "beta")):
                    sp.dma_start(bias[:, i:i + 1], w[name].rearrange("(c o) -> c o", o=1)).then_inc(loaded, 16)
                sp.dma_start(bv_sb[:, :], w["bv"].rearrange("(o c) -> o c", o=1).to_broadcast([128, C])).then_inc(loaded, 16)
                sp.dma_start(id_sb[:, :], w["ident"]).then_inc(loaded, 16)
                sp.wait_ge(zero_ready, 1)
                for b in range(B):
                    for at in (0, W + L):
                        sp.dma_start(z_ext[b, :, at:at + W], heads_out[:, 0, 0:W]).then_inc(loaded, 16)
                sp.wait_ge(loaded, 16 * (11 + 2 * B))

            @block.gpsimd
            def _(pool):
                pool.memset(heads_out[:, 0, 0:W], 0.0).then_inc(zero_ready, 1)
                pool.memset(v_next[:, :, :, D:D + 1], 1.0)
                pool.memset(v_cur[:, :, :, D:D + 1], 1.0)
                pool.memset(eps[:, :], LN_EPS)
                pool.memset(ones_c[:, :], 1.0 / C)

            @block.vector
            def _(dve):
                for buf in range(2):
                    nc.vector.memset(k_st[PARTS:128, buf, :].bitcast(F32), 1.0)
                nc.vector.memset(ps[:, 6:8, :], 0.0)
                nc.vector.memset(sel_o[:, :], 0.0).then_inc(made, 1)
                nc.vector.memset(sel_d[:, :], 0.0).then_inc(made, 1)
                dve.wait_ge(loaded, 16 * (11 + 2 * B))
                dve.wait_ge(made, 2)
                for half in range(2):
                    r = 64 * half
                    nc.vector.tensor_copy(sel_o[r:r + D, :], id_sb[r:r + D, r:r + D])
                    nc.vector.memset(sel_d[r + D:r + D + 1, :], 1.0)
        clear(nc, names)

        q_proj, x_used, split_ready, split_stored, v_ready, psum_read = [
            sem(n) for n in ("q_proj", "x_used", "split_ready", "split_stored", "v_ready", "psum_read")]
        f_ready = sem("f_ready")
        x_even, x_odd, st_even, st_odd = sem("x_even"), sem("x_odd"), sem("st_even"), sem("st_odd")

        def project(b):
            with nc.Block() as block:
                xc = exps[:, 0, :].rearrange("p (a b) -> p a b", a=2)
                full = lambda r, i: work(2 + 2 * r + i)
                hilo = lambda r, i, part: q_dst[:, r, i, part, :]
                q_dst = split_buf

                @block.sync
                def _(sp):
                    sp.sem_inc(x_used, 2)
                    sp.sem_inc(st_even, 16 * 4)
                    sp.sem_inc(st_odd, 16 * 4)
                    with sp.Fori(0, NCH // 2) as k:
                        for r in range(2):
                            sp.wait_ge(x_used, k * 2 + r + 1)
                            sp.dma_start(xc[:, r, :], x[b, :, bass.ts(k * 2 + r, CH)]).then_inc((x_even, x_odd)[r], 16)

                @block.tensor
                def _(pe):
                    with pe.Fori(0, NCH // 2) as k:
                        for r in range(2):
                            c = k * 2 + r
                            pe.wait_ge((x_even, x_odd)[r], 16 * k + 16)
                            pe.wait_ge(psum_read, c + 1)
                            pe.wait_ge(v_ready, c + 1)
                            for i in range(2):
                                nc.tensor.matmul(ps[:, 3 * r + i, :], w_sb[:, i, :], xc[:, r, :],
                                                 start=True, stop=True).then_inc(q_proj, 1)
                            for j in range(CH // 128):
                                last = nc.tensor.matmul(ps[:, 3 * r + 2, 128 * j:128 * j + 128],
                                                        xc[:, r, 128 * j:128 * j + 128], w_sb[:, 2, :],
                                                        start=True, stop=True)
                            last.then_inc(x_used, 1)

                @block.scalar
                def _(act):
                    act.sem_inc(psum_read, 2)
                    with act.Fori(0, NCH // 2) as k:
                        for r in range(2):
                            c = k * 2 + r
                            act.wait_ge(split_ready, c + 1)
                            for i in range(2):
                                act.wait_ge(q_proj, c * 2 + i + 1)
                                ins = nc.scalar.activation(full(r, i), ps[:, 3 * r + i, :], ACT.Identity,
                                                           bias=bias[:, i:i + 1])
                                if i == 0:
                                    ins.then_inc(f_ready, 1)
                            ins.then_inc(psum_read, 1)
                            act.wait_ge(split_ready, c + 3)
                            for i in range(2):
                                for part in range(2):
                                    act.dma_start(qk_split[i, part, :, bass.ts(c, CH)], hilo(r, i, part).bitcast(F32)
                                                  ).then_inc((st_even, st_odd)[r], 16)

                @block.vector
                def _(dve):
                    dve.sem_inc(split_ready, 2)
                    dve.sem_inc(v_ready, 2)
                    with dve.Fori(0, NCH // 2) as k:
                        for r in range(2):
                            c = k * 2 + r
                            dve.wait_ge(x_used, c + 3)
                            vt = v_next[:, :, bass.ts(c, CH // 128), 0:D].rearrange("p h t d -> p t h d")
                            nc.vector.tensor_tensor(
                                vt, ps[:, 3 * r + 2, :].rearrange("p (t h d) -> p t h d", t=CH // 128, d=D),
                                bv_sb[:, :].rearrange("p (o h d) -> p o h d", o=1, d=D).to_broadcast([128, CH // 128, HEADS, D]),
                                ALU.add).then_inc(v_ready, 1)
                            dve.wait_ge((st_even, st_odd)[r], 64 * k + 64)
                            dve.wait_ge(psum_read, c + 3)
                            for i in range(2):
                                nc.vector.tensor_copy(hilo(r, i, 0), full(r, i)).then_inc(made, 1)
                            for i in range(2):
                                dve.wait_ge(made, c * 2 + i + 1)
                                last = nc.vector.tensor_tensor(hilo(r, i, 1), full(r, i), hilo(r, i, 0).bitcast(F32), ALU.subtract)
                            last.then_inc(split_ready, 1)

                @block.gpsimd
                def _(pool):
                    pool.wait_ge(st_even, 64 * (NCH // 2) + 64)
                    pool.wait_ge(st_odd, 64 * (NCH // 2) + 64)
            clear(nc, names)

        k_first, k_rest = sem("k_first"), sem("k_rest")
        q_piece = [sem(f"q_piece{i}") for i in range(NCH)]
        smax_ready, smax_done, sexp_ready, exp_done, av_done, out_read = [
            sem(n) for n in ("smax_ready", "smax_done", "sexp_ready", "exp_done", "av_done", "out_read")]
        mneg_ready, mt_ready, mrow_hi, mrow_ready, mrow_stored = [
            sem(n) for n in ("mneg_ready", "mt_ready", "mrow_hi", "mrow_ready", "mrow_stored")]

        def attend(h, nxt):
            buf, nbuf = (h or 0) % 2 if h is not None else None, nxt % 2 if nxt is not None else None

            def over_chunks(e, part, lead=None):
                if lead:
                    lead()
                with e.Fori(0, NCH // 2 - 1) as k:
                    for r in range(2):
                        part(k * 2 + r, r)
                for r in range(2):
                    part(NCH - 2 + r, r)

            with nc.Block() as block:
                @block.sync
                def _(sp):
                    if nxt is not None:
                        hd = slice(D * nxt, D * nxt + D)

                        def rows(i, c0, c1, sem_):
                            for n, part in enumerate(((0, 1, 0), (0, 0, 1))[i]):
                                sp.dma_start((q_st, k_st)[i][D * n:D * n + D, nbuf, c0 * CH:c1 * CH].bitcast(F32),
                                             qk_split[i, part, hd, c0 * CH:c1 * CH]).then_inc(sem_, 16)
                        rows(1, 0, 1, k_first)
                        rows(0, 0, 1, q_piece[0])
                        rows(0, 1, 2, q_piece[1])
                        rows(1, 1, NCH, k_rest)
                        for c in range(2, NCH):
                            rows(0, c, c + 1, q_piece[c])
                        sp.wait_ge(mrow_ready, 1)
                        for part in range(2):
                            sp.dma_start(q_st[PARTS + part:PARTS + part + 1, nbuf, :].bitcast(F32), mrow[:, part, :].bitcast(F32)).then_inc(mrow_stored, 16)
                        sp.wait_ge(mrow_stored, 32)

                @block.tensor
                def _(pe):
                    def max_tile(c, r, t):
                        if t % (CH // 128) == 0:
                            pe.wait_ge(q_piece[t // (CH // 128)], 48)
                        if t == 0:
                            pe.wait_ge(k_rest if r else k_first, 48)
                        pe.wait_ge(smax_done, c * NT + t + 1)
                        nc.tensor.matmul(ps[:, t % 2, :], q_st[0:PARTS, nbuf, 128 * t:128 * t + 128],
                                         k_st[0:PARTS, nbuf, bass.ts(c, CH)], start=True, stop=True).then_inc(smax_ready, 1)

                    def exp_tile(c, u, i):
                        t = 2 * u + i
                        if i == 0:
                            pe.wait_ge(exp_done, c * PAIRS + u + 1)
                        ins = nc.tensor.matmul(ps[:, 2 + 2 * (u % 2) + i, :], k_st[0:SHIFT, buf, 128 * t:128 * t + 128],
                                               q_st[0:SHIFT, buf, bass.ts(c, CH)], start=True, stop=True)
                        if i:
                            ins.then_inc(sexp_ready, 1)

                    def scores(c, r, u):
                        for i in range(2):
                            if nxt is not None:
                                max_tile(c, r, 2 * u + i)
                            if h is not None:
                                exp_tile(c, u, i)

                    def attn_v(c, r, u):
                        if u == 0:
                            pe.wait_ge(out_read, c + 1)
                        pe.wait_ge(exp_done, c * PAIRS + u + 3)
                        for i in range(2):
                            t = 2 * u + i
                            ins = nc.tensor.matmul(ps[64 * i:64 * i + D + 1, 6 + r, :], v_cur[:, h, t, :],
                                                   exps[:, u % 4, CH * i:CH * i + CH], start=(u == 0), stop=(u == PAIRS - 1))
                        ins.then_inc(av_done, 1)

                    AHEAD = 2

                    def part(c, r):
                        for u in range(PAIRS):
                            if u + AHEAD < PAIRS:
                                scores(c, r, u + AHEAD)
                            elif not isinstance(c, int) or c + 1 < NCH:
                                scores(c + 1, 1 - r, u + AHEAD - PAIRS)
                            if h is not None:
                                attn_v(c, r, u)

                    over_chunks(pe, part, lambda: [scores(0, 0, u) for u in range(AHEAD)])
                    if nxt is not None:
                        pe.wait_ge(mneg_ready, 1)
                        nc.tensor.transpose(ps[0:NT, 0, 0:128], mneg[:, :], id_sb[:, :]).then_inc(mt_ready, 1)

                @block.scalar
                def _(act):
                    if h is None:
                        return
                    act.sem_inc(exp_done, 2)
                    act.sem_inc(out_read, 2)

                    def read_out(c, r):
                        act.wait_ge(av_done, c * PAIRS + PAIRS + 4)
                        nc.scalar.copy(heads_out[:, h, bass.ts(c, CH)], ps[:, 6 + r, :]).then_inc(out_read, 1)

                    def part(c, r):
                        for u in range(PAIRS):
                            n = c * PAIRS + u
                            act.wait_ge(sexp_ready, n + 1)
                            act.wait_ge(av_done, n + 1)
                            nc.scalar.activation(exps[:, u % 4, :], ps[:, 2 + 2 * (u % 2):4 + 2 * (u % 2), :].rearrange("p a b -> p (a b)"),
                                                 ACT.Exp, scale=SCALE).then_inc(exp_done, 1)
                            if u == 3 and (not isinstance(c, int) or c > 0):
                                read_out(c - 1, 1 - r)

                    part(0, 0)
                    with act.Fori(0, NCH // 2 - 1) as k:
                        for r in range(2):
                            part(k * 2 + r + 1, 1 - r)
                    part(NCH - 1, 1)
                    read_out(NCH - 1, 1)

                @block.gpsimd
                def _(pool):
                    if h is not None:
                        pool.sem_inc(av_done, 4)

                @block.vector
                def _(dve):
                    if nxt is None:
                        return
                    dve.sem_inc(smax_done, 2)
                    with dve.Fori(0, NCH) as c:
                        for t in range(NT):
                            dve.wait_ge(smax_ready, c * NT + t + 1)
                            nc.vector.tensor_reduce(mpart[:, c, t:t + 1], ps[:, t % 2, :], AX.X, ALU.max).then_inc(smax_done, 1)
                    dve.wait_ge(smax_done, NCH * NT + 2)
                    nc.vector.tensor_reduce(mneg[:, :], mpart[:, :, :].rearrange("p c t -> p t c"), AX.X, ALU.max,
                                            negate=True).then_inc(mneg_ready, 1)
                    dve.wait_ge(mt_ready, 1)
                    nc.vector.tensor_copy(mrow[:, 0, :], ps[0:NT, 0, 0:128]).then_inc(mrow_hi, 1)
                    dve.wait_ge(mrow_hi, 1)
                    nc.vector.tensor_tensor(mrow[:, 1, :], ps[0:NT, 0, 0:128], mrow[:, 0, :].bitcast(F32), ALU.subtract).then_inc(mrow_ready, 1)
            clear(nc, names)

        def take_v():
            with nc.Block() as block:
                @block.vector
                def _(dve):
                    nc.vector.tensor_copy(v_cur[:, :, :, :], v_next[:, :, :, :])

        (od_ready, log_d, recip_d, normed, wo_ready, y_ready, mean_ready, centred, squared, var_ready, log_v, rstd_ready,
         scaled, z_ready, z_stored) = [sem(n) for n in (
             "od_ready", "log_d", "recip_d", "normed", "wo_ready", "y_ready", "mean_ready", "centred", "squared", "var_ready", "log_v",
             "rstd_ready", "scaled", "z_ready", "z_stored")]

        def finish(b):
            X_IN, RECIP, NORMED, Y, CENTRED, SQUARE, RSTD = range(7)
            buf = lambda what, r: work(2 * what + r)
            Z, SCALED = range(2)
            with nc.Block() as block:
                @block.sync
                def _(sp):
                    sp.sem_inc(y_ready, 2)
                    with sp.Fori(0, NCH // 2) as k:
                        for r in range(2):
                            c = k * 2 + r
                            sp.wait_ge(y_ready, c + 1)
                            sp.dma_start(buf(X_IN, r), x[b, :, bass.ts(c, CH)]).then_inc((x_even, x_odd)[r], 16)
                    sp.wait_ge(z_ready, NCH)
                    sp.dma_start(z_ext[b, :, W:W + L], heads_out[:, Z, :]).then_inc(z_stored, 16)
                    sp.wait_ge(z_stored, 16)

                @block.tensor
                def _(pe):
                    for step in range(NCH + 3):
                        c = step
                        if c < NCH:
                            pe.wait_ge(normed, c + 1)
                            for sel, bank in ((sel_o, 0), (sel_d, 1)):
                                for h in range(HEADS):
                                    ins = nc.tensor.matmul(ps[D * h:D * h + D, bank, :], sel[:, :],
                                                           heads_out[:, h, c * CH:c * CH + CH], start=True, stop=True)
                            ins.then_inc(od_ready, 1)
                        c, r = step - 1, (step - 1) % 2
                        if 0 <= c < NCH:
                            pe.wait_ge(normed, c + 2)
                            pe.wait_ge(y_ready, c + 1)
                            nc.tensor.matmul(ps[:, 2 + r, :], w_sb[:, 3, :], buf(NORMED, r), start=True, stop=True).then_inc(wo_ready, 1)
                        c, r = step - 2, step % 2
                        if 0 <= c < NCH:
                            pe.wait_ge(y_ready, c + 3)
                            pe.wait_ge(centred, c + 1)
                            nc.tensor.matmul(ps[:, 4 + r, :], ones_c[:, :], buf(Y, r), start=True, stop=True).then_inc(mean_ready, 1)
                        c, r = step - 3, (step - 3) % 2
                        if 0 <= c < NCH:
                            pe.wait_ge(squared, c + 1)
                            pe.wait_ge(rstd_ready, c + 1)
                            nc.tensor.matmul(ps[:, 6 + r, :], ones_c[:, :], buf(SQUARE, r), start=True, stop=True).then_inc(var_ready, 1)

                @block.scalar
                def _(act):
                    act.sem_inc(rstd_ready, 2)

                    def emit(step, par, stages):
                        if 0 in stages:
                            c, r = step, par
                            act.wait_ge(od_ready, c + 1)
                            act.wait_ge(normed, c + 1)
                            nc.scalar.activation(buf(RECIP, r), ps[:, 1, :], ACT.Ln).then_inc(log_d, 1)
                            act.wait_ge(log_d, c + 1)
                            nc.scalar.activation(buf(RECIP, r), buf(RECIP, r), ACT.Exp, scale=-1.0).then_inc(recip_d, 1)
                        if 2 in stages:
                            c, r = step - 2, par
                            act.wait_ge(centred, c + 3)
                            nc.scalar.activation(buf(SQUARE, r), buf(CENTRED, r), ACT.Square).then_inc(squared, 1)
                        if 3 in stages:
                            c, r = step - 3, (par - 3) % 2
                            act.wait_ge(var_ready, c + 1)
                            act.wait_ge(scaled, c + 1)
                            nc.scalar.activation(buf(RSTD, r), ps[:, 6 + r, :], ACT.Ln, bias=eps[:, 0:1]).then_inc(log_v, 1)
                            act.wait_ge(log_v, c + 1)
                            nc.scalar.activation(buf(RSTD, r), buf(RSTD, r), ACT.Exp, scale=-0.5).then_inc(rstd_ready, 1)
                        if 4 in stages:
                            c = step - 4
                            act.wait_ge(scaled, c + 3)
                            nc.scalar.activation(heads_out[:, Z, bass.ts(c, CH)], heads_out[:, SCALED, bass.ts(c, CH)], ACT.Identity,
                                                 bias=bias[:, 4:5], scale=bias[:, 3:4]).then_inc(z_ready, 1)
                    pipelined(act, NCH, 5, emit)

                @block.vector
                def _(dve):
                    dve.sem_inc(normed, 1)
                    dve.sem_inc(centred, 2)
                    dve.sem_inc(scaled, 2)

                    def emit(step, par, stages):
                        if 0 in stages:
                            c, r = step, par
                            dve.wait_ge(recip_d, c + 1)
                            nc.vector.tensor_tensor(buf(NORMED, r), ps[:, 0, :], buf(RECIP, r), ALU.mult).then_inc(normed, 1)
                        if 1 in stages:
                            c, r = step - 1, (par - 1) % 2
                            dve.wait_ge((x_even, x_odd)[r], (c - r) * 8 + 16)
                            dve.wait_ge(wo_ready, c + 1)
                            nc.vector.scalar_tensor_tensor(buf(Y, r), ps[:, 2 + r, :], bias[:, 2:3], buf(X_IN, r), ALU.add, ALU.add
                                                           ).then_inc(y_ready, 1)
                        if 2 in stages:
                            c, r = step - 2, par
                            dve.wait_ge(mean_ready, c + 1)
                            dve.wait_ge(scaled, c + 1)
                            nc.vector.tensor_tensor(buf(CENTRED, r), buf(Y, r), ps[:, 4 + r, :], ALU.subtract).then_inc(centred, 1)
                        if 3 in stages:
                            c, r = step - 3, (par - 3) % 2
                            dve.wait_ge(rstd_ready, c + 3)
                            nc.vector.tensor_tensor(heads_out[:, SCALED, bass.ts(c, CH)], buf(CENTRED, r), buf(RSTD, r), ALU.mult
                                                    ).then_inc(scaled, 1)
                    pipelined(dve, NCH, 4, emit)
            clear(nc, names)

        def batch(b, last):
            take_v()
            for h in range(HEADS):
                if h == HEADS - 1:
                    if not last:
                        project(b + 1)
                    attend(h, None if last else 0)
                else:
                    attend(h, h + 1)
            finish(b)

        project(0)
        attend(None, 0)
        if nb > 1:
            with nc.Fori(0, nb - 1) as b:
                batch(b, False)
        batch(nb - 1, True)


ST = 16
GC = 128 // ST
INNER = 2 * C
LN_EXP = "natural_log_exp_and_others"
LC = 512
STEPS = L // LC
ROWS = LC // W
HALO = (ROWS + 2) * W
GROUPS = INNER // GC
RANK = 8


def layer1(nc, z_ext, w, out, nb=B):
    NIT = nb * STEPS
    with ExitStack() as ctx:
        def sb(name, shape, dt=F32):
            return ctx.enter_context(nc.sbuf_tensor(name, shape, dt))

        names = []

        def sem(name):
            s = ctx.enter_context(nc.semaphore(name))
            names.append(s)
            return s

        ps = ctx.enter_context(nc.psum_tensor("ps1", [128, 8, CH], F32))
        DT_BANK, U_BANK, Y_BANK, O_BANK, ITEM_BANK = 0, 2, 4, 5, 6
        win = sb("win", [C, 2 * INNER])
        wtap = sb("wtap", [C, 4, INNER])
        wxd = sb("wxd", [128, 2, 128])
        wdt = sb("wdt", [128, INNER])
        sel_b = sb("sel_b", [128, 128])
        sel_c = sb("sel_c", [128, 128])
        sel_g = sb("sel_g", [128, 8, 128], F32R)
        sel_y = sb("sel_y", [128, 4, 32])
        wconv = sb("wconv", [C, 9, C])
        wspec = sb("wspec", [C, 4, C])
        wmix = sb("wmix", [C, 4, C])
        hilb = sb("hilb", [128, 128])
        wout = sb("wout", [128, 2, C])
        cols = sb("cols", [128, 9])
        a_neg = sb("a_neg", [128, GROUPS])
        carry = sb("carry", [128, STEPS + 1, GROUPS])
        row0 = sb("row0", [128, STEPS, W])
        hil0 = sb("hil0", [128, W])
        za = sb("za", [128, 2, HALO])
        zp = sb("zp", [128, 2, ROWS + 2, W + 2])
        zj = sb("zj", [128, 2, LC])
        xs = sb("xs", [128, 2, 2, LC])
        gz = sb("gz", [128, 2, 2, LC])
        s_dt = sb("s_dt", [128, 2, 4, LC], F32R)
        s_u = sb("s_u", [128, 2, 4, LC], F32R)
        b_rep = sb("b_rep", [128, 2, LC])
        c_rep = sb("c_rep", [128, 2, LC])
        g_t = sb("g_t", [128, 2, LC])
        o_sb = sb("o_sb", [128, 2, LC])
        stage_j = sb("stage_j", [128, ROWS, W])
        edt = sb("edt", [128, 2, LC])
        dt = sb("dt", [128, 2, LC])
        ux = sb("ux", [128, 2, LC])
        xd = sb("xd", [128, LC])
        yt = sb("yt", [128, 2, LC])
        NDA, NBU, NHH, NHC = 8, 4, 8, 8
        d_a = sb("d_a", [128, NDA, LC])
        b_u = sb("b_u", [128, NBU, LC])
        hh = sb("hh", [128, NHH, LC])
        hc = sb("hc", [128, NHC, LC])

        loaded, mixed, a_exp, carry_zero, row_zero, halved = [sem(n) for n in (
            "loaded1", "mixed", "a_exp", "carry_zero", "row_zero", "halved")]
        NLOAD = 15 * 16
        with nc.Block() as block:
            @block.sync
            def _(sp):
                for dst, src in (
                        (win[:, :], w["win"]), (xs[:, :, :, :].rearrange("p a b c -> p (a b c)")[:, 0:4 * INNER],
                                                w["taps"].rearrange("(o k) e -> o (k e)", o=1).to_broadcast([C, 4 * INNER])),
                        (wxd[:, :, :], w["wxd"]), (wdt[:, :], w["wdt"]), (sel_b[:, :], w["sel_b"]), (sel_c[:, :], w["sel_c"]),
                        (hh[:, 0:2, :].rearrange("p a b -> p (a b)"), w["sel_g"]), (sel_y[:, :, :], w["sel_y"]),
                        (wconv[:, :, :], w["wconv"]), (wspec[:, :, :], w["wspec"]), (hilb[:, :], w["hilb"]),
                        (hil0[:, :], w["hil0"].to_broadcast([128, W])), (wout[:, :, :], w["wout"]), (cols[:, :], w["cols"]),
                        (a_neg[:, :], w["a_log"])):
                    sp.dma_start(dst, src).then_inc(loaded, 16)
                sp.wait_ge(loaded, NLOAD)

            @block.gpsimd
            def _(pool):
                pool.memset(zp[:, :, :, :], 0.0)
                pool.memset(carry[:, :, :], 0.0)
                pool.memset(row0[:, :, :], 0.0).then_inc(row_zero, 1)

            @block.scalar
            def _(act):
                act.wait_ge(loaded, NLOAD)
                nc.scalar.activation(a_neg[:, :], a_neg[:, :], ACT.Exp).then_inc(a_exp, 1)
                act.wait_ge(a_exp, 1)
                nc.scalar.mul(a_neg[:, :], a_neg[:, :], -1.0)

            @block.vector
            def _(dve):
                dve.wait_ge(loaded, NLOAD)
                nc.vector.tensor_copy(sel_g[:, :, :].rearrange("p a b -> p (a b)"), hh[:, 0:2, :].rearrange("p a b -> p (a b)"))
                nc.vector.tensor_tensor(wtap[:, :, :],
                                        xs[:, :, :, :].rearrange("p a b c -> p (a b c)")[:, 0:4 * INNER].rearrange("p (k e) -> p k e", k=4),
                                        win[:, 0:INNER].rearrange("p (o e) -> p o e", o=1).to_broadcast([C, 4, INNER]), ALU.mult)
                RR, RI, IR, II = range(4)
                nc.vector.tensor_tensor(wmix[:, 0, :], wspec[:, RR, :], wspec[:, II, :], ALU.add)
                nc.vector.tensor_tensor(wmix[:, 1, :], wspec[:, RR, :], wspec[:, II, :], ALU.subtract)
                nc.vector.tensor_tensor(wmix[:, 2, :], wspec[:, IR, :], wspec[:, RI, :], ALU.subtract)
                nc.vector.tensor_tensor(wmix[:, 3, :], wspec[:, IR, :], wspec[:, RI, :], ALU.add).then_inc(mixed, 1)
                dve.wait_ge(mixed, 1)
                nc.vector.tensor_scalar_mul(wmix[:, :, :], wmix[:, :, :], 0.5).then_inc(halved, 1)
                dve.wait_ge(row_zero, 1)
                nc.vector.tensor_scalar(row0[:, 0, :], hil0[:, :], cols[:, 8:9], None, ALU.mult).then_inc(halved, 1)
                dve.wait_ge(halved, 2)
                nc.vector.tensor_tensor(wconv[:, 4, :], wconv[:, 4, :], wmix[:, 0, :], ALU.add)
                nc.vector.tensor_tensor(row0[:, 0, 0:1], row0[:, 0, 0:1], cols[:, 7:8], ALU.add)
        clear(nc, names)

        (z_in, flipped, item, item_read, sp_log, dt_sum, u_prod, hi_ready, lo_ready,
         dt_rep, u_rep, da_ready, bu_ready, scanned, kept, hc_ready, y_done, y_added, gated, z_used, o_ready, o_copied,
         o_full, o_even, o_odd) = [sem(x) for x in (
             "z_in", "flipped", "item", "item_read", "sp_log", "dt_sum", "u_prod",
             "hi_ready", "lo_ready", "dt_rep", "u_rep", "da_ready", "bu_ready", "scanned", "kept", "hc_ready", "y_done",
             "y_added", "gated", "z_used", "o_ready", "o_copied", "o_full", "o_even", "o_odd")]

        XS, XD, DT, BI, CI, GATE, GI, NITEM = 0, 2, 3, 5, 6, 7, 9, 10
        G = GROUPS
        LEAD = 4

        def ge(e, s, value):
            if not isinstance(value, int) or value > 0:
                e.wait_ge(s, value)

        def column(g):
            half, jj, i = g // 16, g // 4 % 4, g % 4
            return 2 * half + i // 2, jj + 4 * (i % 2)

        def steps(e, prepare, emit, tail):
            for g in range(G):
                prepare(0, 0, g)
            for it in range(2):
                emit(it, it)
            with e.Fori(1, NIT // 2) as k:
                for r in range(2):
                    emit(k * 2 + r, r)
            tail()

        with nc.Block() as block:
            @block.sync
            def _(sp):
                def load(j, p):
                    jw = j if isinstance(j, int) else j % NIT
                    b, lc = jw // STEPS, jw % STEPS
                    ge(sp, z_used, j - 1)
                    ge(sp, flipped, 2 * j)
                    sp.dma_start(za[:, p, :], z_ext[b, :, bass.ds(lc * LC, HALO)]).then_inc(z_in, 16)
                    sp.dma_start(zp[:, p, :, 1:W + 1], z_ext[b, :, bass.ds(lc * LC, HALO)].rearrange("c (h w) -> c h w", w=W)).then_inc(z_in, 16)
                    last = (STEPS - 1 - lc) * LC + W
                    sp.dma_start(stage_j[:, 0:ROWS - 1, :], z_ext[b, :, bass.ds(last + W, LC - W)].rearrange("c (h w) -> c h w", w=W)).then_inc(z_in, 16)
                    sp.dma_start(stage_j[:, ROWS - 1, :], z_ext[b, :, bass.ds((STEPS - lc) % STEPS * LC + W, W)]).then_inc(z_in, 16)

                def store(j, p):
                    b, lc = j // STEPS, j % STEPS
                    sp.wait_ge(o_full, j + 1)
                    sp.dma_start(out[b, :, bass.ds(lc * LC, LC)], o_sb[:, p, :]).then_inc((o_even, o_odd)[p], 16)

                load(0, 0)
                load(1, 1)
                load(2, 0)
                with sp.Fori(1, NIT // 2) as k:
                    store(k * 2 - 2, 0)
                    load(k * 2 + 1, 1)
                    store(k * 2 - 1, 1)
                    load(k * 2 + 2, 0)
                store(NIT - 2, 0)
                store(NIT - 1, 1)
                sp.wait_ge(o_even, 16 * (NIT // 2))
                sp.wait_ge(o_odd, 16 * (NIT // 2))
                sp.wait_ge(z_in, 64 * (NIT + 1))

            @block.tensor
            def _(pe):
                def bank(n):
                    return ps[:, ITEM_BANK + n % 2, :]

                def begin(j, n):
                    ge(pe, item_read, j * NITEM + n - 1)

                def prepare(j, p, g):
                    if 1 <= g <= 7:
                        if g == 1:
                            pe.wait_ge(z_in, j * 64 + 64)
                        for n in (g - 1,) if g < 7 else (6, 7):
                            h, k = n // 4, n % 4
                            if k == 0:
                                begin(j, XS + h)
                            ins = nc.tensor.matmul(bank(XS + h), wtap[:, k, 128 * h:128 * h + 128],
                                                   za[:, p, W - 3 + k:W - 3 + k + LC], start=(k == 0), stop=(k == 3))
                            if k == 3:
                                ins.then_inc(item, 1)
                    elif g in (11, 12):
                        i = g - 11
                        if i == 0:
                            begin(j, XD)
                            pe.wait_ge(item_read, j * NITEM + XS + 2)
                        ins = nc.tensor.matmul(bank(XD), wxd[:, i, :], xs[:, p, i, :], start=(i == 0), stop=(i == 1))
                        if i == 1:
                            ins.then_inc(item, 1)
                    elif g in (15, 16):
                        n = DT + g - 15
                        begin(j, n)
                        pe.wait_ge(item_read, j * NITEM + XD + 1)
                        nc.tensor.matmul(bank(n), wdt[:, 128 * (g - 15):128 * (g - 15) + 128], xd[:, :], start=True, stop=True
                                         ).then_inc(item, 1)
                    elif g in (19, 20):
                        n = BI + g - 19
                        begin(j, n)
                        nc.tensor.matmul(bank(n), (sel_b, sel_c)[g - 19][:, :], xd[:, :], start=True, stop=True).then_inc(item, 1)
                    elif g in (22, 23):
                        n, h = GATE + g - 22, g - 22
                        begin(j, n)
                        nc.tensor.matmul(bank(n), win[:, INNER + 128 * h:INNER + 128 * h + 128], za[:, p, W:W + LC],
                                         start=True, stop=True).then_inc(item, 1)
                    elif g == 29:
                        begin(j, GI)
                        pe.wait_ge(flipped, j * 2 + 2)
                        for i in range(LC // 128):
                            o = bank(GI)[:, 128 * i:128 * i + 128]
                            nc.tensor.matmul(o, za[:, p, W + 128 * i:W + 128 * i + 128], wmix[:, 2, :], start=True, stop=False)
                            ins = nc.tensor.matmul(o, zj[:, p, 128 * i:128 * i + 128], wmix[:, 3, :], start=False, stop=True)
                        ins.then_inc(item, 1)

                def fill(it, p, n):
                    o = ps[:, O_BANK, :]
                    if n < 9:
                        if n == 0:
                            ge(pe, o_copied, it)
                        dy, dx = n // 3, n % 3
                        nc.tensor.matmul(o.rearrange("p (a b) -> p a b", b=W), wconv[:, n, :], zp[:, p, dy:dy + ROWS, dx:dx + W],
                                         start=(n == 0), stop=False)
                    else:
                        nc.tensor.matmul(o, wmix[:, 1, :], zj[:, p, :], start=False, stop=False).then_inc(z_used, 1)

                def fill_g(it, p):
                    for i in range(LC // 128):
                        nc.tensor.matmul(ps[:, O_BANK, 128 * i:128 * i + 128], g_t[:, p, 128 * i:128 * i + 128], hilb[:, :],
                                         start=False, stop=False)

                def sum_states(it, n):
                    pe.wait_ge(hc_ready, it * G + 4 * n + 4)
                    if n % 4 == 0:
                        ge(pe, y_added, it * 2 + n // 4)
                    for i in range(4):
                        ins = nc.tensor.matmul(ps[32 * i:32 * i + 32, Y_BANK, :], sel_y[:, n % 4, :], hc[:, (4 * n + i) % NHC, :],
                                               start=(n % 4 == 0), stop=(n % 4 == 3))
                    ins.then_inc(y_done, 1)

                def out_proj(it, i):
                    if i == 0:
                        pe.wait_ge(gated, it * 2 + 2)
                    ins = nc.tensor.matmul(ps[:, O_BANK, :], wout[:, i, :], yt[:, i, :], start=False, stop=(i == 1))
                    if i == 1:
                        ins.then_inc(o_ready, 1)

                def repeat_dt(it, p, g):
                    s, j = column(g)
                    if g == 0:
                        pe.wait_ge(lo_ready, it * 4 + 2)
                    ge(pe, da_ready, it * G + g - 1)
                    nc.tensor.matmul(ps[:, DT_BANK + g % 2, :], sel_g[:, j, :], s_dt[:, p, s, :], start=True, stop=True).then_inc(dt_rep, 1)

                def repeat_u(it, p, g):
                    s, j = column(g)
                    if g == 0:
                        pe.wait_ge(lo_ready, it * 4 + 4)
                    ge(pe, bu_ready, it * G + g - 1)
                    nc.tensor.matmul(ps[:, U_BANK + g % 2, :], sel_g[:, j, :], s_u[:, p, s, :], start=True, stop=True).then_inc(u_rep, 1)

                FILLS = (18, 21, 21, 24, 24, 25, 26, 27, 27, 28)

                def emit(it, p):
                    for g in range(G):
                        if isinstance(it, int) and it == g == 0:
                            for d in range(LEAD):
                                repeat_dt(it, p, d)
                        repeat_u(it, p, g)
                        prepare(it + 1, 1 - p, g)
                        if g in (0, 4) and not (isinstance(it, int) and it == 0):
                            sum_states(it - 1, 6 + g // 4)
                        if g in (13, 14) and not (isinstance(it, int) and it == 0):
                            out_proj(it - 1, g - 13)
                        for n in range(10):
                            if FILLS[n] == g:
                                fill(it, p, n)
                        if g == 30:
                            fill_g(it, p)
                        if g >= 8 and g % 4 == 0:
                            sum_states(it, g // 4 - 2)
                        if g + LEAD < G:
                            repeat_dt(it, p, g + LEAD)
                        else:
                            repeat_dt(it + 1, 1 - p, g + LEAD - G)

                def tail():
                    sum_states(NIT - 1, 6)
                    sum_states(NIT - 1, 7)
                    for i in range(2):
                        out_proj(NIT - 1, i)
                steps(pe, prepare, emit, tail)

            @block.scalar
            def _(act):
                def take(j, n):
                    act.wait_ge(item, j * NITEM + n + 1)
                    return ps[:, ITEM_BANK + n % 2, :]

                def silus(dst, j, n, bias):
                    for h in range(2):
                        nc.scalar.activation(dst[:, h, :], take(j, n + h), ACT.Silu, bias=bias(h)).then_inc(item_read, 1)
                    nc.scalar.preload_act_table_set(LN_EXP)

                def high(j, p, stack, src, part):
                    a = slice(64 * part, 64 * part + 64)
                    nc.scalar.copy(stack[a, p, part::2, :], src[a, :, :]).then_inc(hi_ready, 1)

                def prepare(j, p, g):
                    if g == 3:
                        act.wait_ge(z_in, j * 64 + 64)
                        zf = zj[:, p, :].rearrange("p (h w) -> p h w", w=W)
                        nc.scalar.copy(zf[:, :, 0:1], stage_j[:, ::-1, 0:1]).then_inc(flipped, 1)
                        nc.scalar.copy(zf[:, :, 1:W], stage_j[:, ::-1, W - 1:0:-1]).then_inc(flipped, 1)
                    elif g == 10:
                        ge(act, y_added, j * 2 - 2)
                        silus(xs[:, p, :, :], j, XS, lambda h: cols[:, h:h + 1])
                    elif g == 15:
                        nc.scalar.copy(xd[:, :], take(j, XD)).then_inc(item_read, 1)
                    elif g in (19, 20):
                        h = g - 19
                        if h == 0:
                            ge(act, lo_ready, j * 4)
                        nc.scalar.activation(dt[:, h, :], take(j, DT + h), ACT.Relu, bias=cols[:, 2 + h:3 + h])
                        nc.scalar.activation(edt[:, h, :], take(j, DT + h), ACT.Abs, bias=cols[:, 2 + h:3 + h]).then_inc(item_read, 1)
                    elif g == 21:
                        act.wait_ge(item_read, j * NITEM + DT + 2)
                        nc.scalar.activation(edt[:, :, :], edt[:, :, :], ACT.Exp, scale=-1.0).then_inc(sp_log, 1)
                    elif g == 22:
                        act.wait_ge(sp_log, j * 2 + 1)
                        nc.scalar.activation(edt[:, :, :], edt[:, :, :], ACT.Ln, bias=1.0).then_inc(sp_log, 1)
                    elif g in (23, 24):
                        nc.scalar.copy((b_rep, c_rep)[g - 23][:, p, :], take(j, BI + g - 23)).then_inc(item_read, 1)
                    elif g in (25, 26):
                        act.wait_ge(dt_sum, j + 1)
                        high(j, p, s_dt, dt, g - 25)
                    elif g in (27, 28):
                        act.wait_ge(u_prod, j + 1)
                        high(j, p, s_u, ux, g - 27)
                    elif g == 29:
                        ge(act, gated, j * 2 - 2)
                        silus(gz[:, p, :, :], j, GATE, lambda h: 0.0)
                    elif g == 31:
                        nc.scalar.copy(g_t[:, p, :], take(j, GI)).then_inc(item_read, 1)

                KEEP = 5

                def last_state(it, p, g):
                    act.wait_ge(scanned, it * G + g + 1)
                    s, j = column(g)
                    nc.scalar.copy(carry[:, it % STEPS + 1, s * 8 + j:s * 8 + j + 1],
                                   hh[:, g % NHH, LC - 1:LC]).then_inc(kept, 1)

                def decay(it, g):
                    s, j = column(g)
                    act.wait_ge(dt_rep, it * G + g + 1)
                    ge(act, scanned, it * G + g - NDA + 1)
                    nc.scalar.activation(d_a[:, g % NDA, :], ps[:, DT_BANK + g % 2, :], ACT.Exp,
                                         scale=a_neg[:, s * 8 + j:s * 8 + j + 1]).then_inc(da_ready, 1)

                def emit(it, p):
                    for g in range(G):
                        decay(it, g)
                        if g >= KEEP:
                            last_state(it, p, g - KEEP)
                        elif not (isinstance(it, int) and it == 0):
                            last_state(it - 1, 1 - p, G + g - KEEP)
                        prepare(it + 1, 1 - p, g)
                        if g == 17 and not (isinstance(it, int) and it == 0):
                            output(it - 1, 1 - p)

                def output(it, p):
                    act.wait_ge(o_ready, it + 1)
                    if not (isinstance(it, int) and it < 2):
                        act.wait_ge((o_even, o_odd)[p], (it - p) * 8)
                    nc.scalar.activation(o_sb[:, p, :], ps[:, O_BANK, :], ACT.Identity, bias=cols[:, 6:7]).then_inc(o_copied, 1)

                def tail():
                    for g in range(LEAD - 2):
                        decay(NIT, g)
                    for g in range(G - KEEP, G):
                        last_state(NIT - 1, 1, g)
                    output(NIT - 1, 1)
                nc.scalar.preload_act_table_set(LN_EXP)
                steps(act, prepare, emit, tail)

            @block.vector
            def _(dve):
                def low(j, p, stack, src, part, n):
                    a, b = slice(64 * part, 64 * part + 64), slice(64 - 64 * part, 128 - 64 * part)
                    dve.wait_ge(hi_ready, j * 4 + 2 * n + part + 1)
                    nc.vector.tensor_tensor(stack[b, p, part::2, :], src[a, :, :], stack[a, p, part::2, :].bitcast(F32), ALU.subtract
                                            ).then_inc(lo_ready, 1)

                def prepare(j, p, g):
                    if g == 20:
                        dve.wait_ge(sp_log, j * 2 + 2)
                        nc.vector.tensor_tensor(dt[:, :, :], dt[:, :, :], edt[:, :, :], ALU.add).then_inc(dt_sum, 1)
                    elif g == 21:
                        dve.wait_ge(dt_sum, j + 1)
                        nc.vector.tensor_tensor(ux[:, :, :], dt[:, :, :], xs[:, p, :, :], ALU.mult).then_inc(u_prod, 1)
                    elif g in (25, 26):
                        low(j, p, s_dt, dt, g - 25, 0)
                    elif g in (27, 28):
                        low(j, p, s_u, ux, g - 27, 1)

                def add_skip(it, p, half):
                    dve.wait_ge(y_done, it * 8 + 4 * half + 4)
                    ge(dve, o_ready, it)
                    nc.vector.scalar_tensor_tensor(yt[:, half, :], xs[:, p, half, :], cols[:, 4 + half:5 + half], ps[:, Y_BANK, :],
                                                   ALU.mult, ALU.add).then_inc(y_added, 1)

                def add_row(it, p):
                    dve.wait_ge(o_copied, it + 1)
                    nc.vector.tensor_tensor(o_sb[:, p, 0:W], o_sb[:, p, 0:W], row0[:, it % STEPS, :], ALU.add).then_inc(o_full, 1)

                def times_b(it, p, g):
                    dve.wait_ge(u_rep, it * G + g + 1)
                    if g == 0:
                        dve.wait_ge(item_read, it * NITEM + BI + 1)
                    ge(dve, scanned, it * G + g - NBU + 1)
                    nc.vector.tensor_tensor(b_u[:, g % NBU, :], ps[:, U_BANK + g % 2, :], b_rep[:, p, :], ALU.mult).then_inc(bu_ready, 1)

                def emit(it, p):
                    times_b(it, p, 0)
                    for g in range(G):
                        if g + 1 < G:
                            times_b(it, p, g + 1)
                        s, j = column(g)
                        dve.wait_ge(bu_ready, it * G + g + 1)
                        dve.wait_ge(da_ready, it * G + g + 1)
                        ge(dve, hc_ready, it * G + g - NHH + 1)
                        ge(dve, kept, it * G + g - NHH + 1)
                        nc.vector.tensor_tensor_scan(hh[:, g % NHH, :], d_a[:, g % NDA, :], b_u[:, g % NBU, :],
                                                     carry[:, it % STEPS, s * 8 + j:s * 8 + j + 1], ALU.mult, ALU.add).then_inc(scanned, 1)
                        prepare(it + 1, 1 - p, g)
                        if g == 21:
                            add_skip(it, p, 0)
                        if not (isinstance(it, int) and it == 0):
                            if g == 5:
                                add_skip(it - 1, 1 - p, 1)
                            if g == 16:
                                add_row(it - 1, 1 - p)

                def tail():
                    add_skip(NIT - 1, 1, 1)
                    add_row(NIT - 1, 1)
                steps(dve, prepare, emit, tail)

            @block.gpsimd
            def _(pool):
                def prepare(j, p, g):
                    pass

                def gate(it, p, half):
                    pool.wait_ge(y_added, it * 2 + half + 1)
                    pool.tensor_tensor(yt[:, half, :], yt[:, half, :], gz[:, p, half, :], ALU.mult).then_inc(gated, 1)

                def emit(it, p):
                    for g in range(G):
                        pool.wait_ge(scanned, it * G + g + 1)
                        if g == 0:
                            pool.wait_ge(item_read, it * NITEM + CI + 1)
                        ge(pool, y_done, it * 8 + (g - NHC) // 4 + 1)
                        pool.tensor_tensor(hc[:, g % NHC, :], hh[:, g % NHH, :], c_rep[:, p, :], ALU.mult).then_inc(hc_ready, 1)
                        prepare(it + 1, 1 - p, g)
                        if g == 22:
                            gate(it, p, 0)
                        if g == 6 and not (isinstance(it, int) and it == 0):
                            gate(it - 1, 1 - p, 1)

                def tail():
                    gate(NIT - 1, 1, 1)
                steps(pool, prepare, emit, tail)
        clear(nc, names)


def hilbert():
    s = np.zeros(W)
    s[1:W // 2], s[W // 2 + 1:] = 1, -1
    return np.real(np.fft.ifft(1j * s[:, None] * np.fft.fft(np.eye(W), axis=0), axis=0))


def host(i):
    f = np.float32
    c = np.ascontiguousarray
    w = {}
    w["win"] = c(i["L1_conv_in_proj_w"].T)
    w["taps"] = c(i["L1_conv_conv1d_w"][:, 0, :].T)
    xp = i["L1_conv_x_proj_w"]
    wx = np.zeros((128, 2, 128), f)
    wx[:, :, :40] = xp.reshape(40, 2, 128).transpose(2, 1, 0)
    w["wxd"] = wx
    wd = np.zeros((128, INNER), f)
    wd[:RANK] = i["L1_conv_dt_proj_w"].T
    w["wdt"] = wd
    p = np.arange(128)
    for name, off in (("sel_b", RANK), ("sel_c", RANK + ST)):
        m = np.zeros((128, 128), f)
        m[off + p % ST, p] = 1
        w[name] = m
    m = np.zeros((128, 8, 128), f)
    for j in range(8):
        for h in range(2):
            m[64 * h + 8 * j + p // ST, j, p] = 1
    w["sel_g"] = m.reshape(128, 1024)
    m = np.zeros((128, 4, 32), f)
    for j in range(4):
        m[p, j, 8 * j + p // ST] = 1
    w["sel_y"] = m
    w["wconv"] = c(i["L1_conv_conv_spatial_w"].reshape(C, C, 9).transpose(1, 2, 0))
    s = i["L1_conv_conv_spectral_w"][:, :, 0, 0].T
    w["wspec"] = c(np.stack([s[:C, :C], s[C:, :C], s[:C, C:], s[C:, C:]], 1))
    hm = hilbert()
    w["hilb"] = np.kron(np.eye(2), hm.T).astype(f)
    w["hil0"] = c(hm[:, 0][None]).astype(f)
    w["wout"] = c(i["L1_conv_out_proj_w"].reshape(C, 2, 128).transpose(2, 1, 0))
    two = lambda v: v.reshape(2, 128).T
    w["cols"] = c(np.concatenate([two(i["L1_conv_conv1d_b"]), two(i["L1_conv_dt_proj_b"]), two(i["L1_conv_D"]),
                                  i["L1_conv_conv_spatial_b"][:, None], two(i["L1_conv_conv_spectral_b"])], 1))
    w["a_log"] = c(i["L1_conv_A_log"].reshape(GROUPS, 128).T)
    return w


def build(nc, x, l0, w, out):
    z_ext = nc.dram_tensor("z_ext", [B, C, L + 2 * W], F32, kind="Internal").ap()
    layer0(nc, x, l0, z_ext)
    layer1(nc, z_ext, w, out)


def kernel(**inputs):
    import concourse.bacc as bacc
    from concourse.bass_utils import run_bass_kernel_spmd

    i = {k: np.asarray(v) for k, v in inputs.items()}
    l0 = {n: i["L0_conv_" + n] for n in ("Wq", "bq", "Wk", "bk", "Wv", "bv", "Wo", "bo", "gamma", "beta")}
    l0["ident"] = np.eye(128, dtype=np.float32)
    w = host(i)
    arrays = {"in_x": np.ascontiguousarray(i["x"].reshape(B, C, L))}
    arrays.update({"in_" + n: np.ascontiguousarray(v) for n, v in l0.items()})
    arrays.update({"in_" + n: np.ascontiguousarray(v) for n, v in w.items()})
    nc = bacc.Bacc("TRN2", target_bir_lowering=False, num_devices=1)
    aps = {n: nc.dram_tensor(n, v.shape, mybir.dt.from_np(v.dtype), kind="ExternalInput").ap() for n, v in arrays.items()}
    out = nc.dram_tensor("out", (B, C, L), F32, kind="ExternalOutput").ap()
    build(nc, aps["in_x"], {n: aps["in_" + n] for n in l0}, {n: aps["in_" + n] for n in w}, out)
    r = run_bass_kernel_spmd(nc, [arrays], core_ids=[0])
    return r.results[0]["out"].reshape(B, C, H, W)
```

```python
import numpy as np
import concourse.bass as bass
import concourse.mybir as mybir
from contextlib import ExitStack

F32, F32R = mybir.dt.float32, mybir.dt.float32r
ACT = mybir.ActivationFunctionType
ALU = mybir.AluOpType
AX = mybir.AxisListType

B, C, H, W = 4, 128, 64, 64
L = H * W
HEADS = 4
D = C // HEADS
SCALE = D ** -0.5
CH = 512
NCH = L // CH
NT = L // 128
PAIRS = NT // 2
QUADS = NT // 4
LN_EPS = 1e-5
LN_EXP = "natural_log_exp_and_others"
PARTS = 3 * D
SHIFT = PARTS + 2


def pipelined(e, n, depth, emit):
    lead = depth - 1 + (depth - 1) % 2
    for step in range(lead):
        emit(step, step % 2, [s for s in range(depth) if 0 <= step - s < n])
    with e.Fori(lead // 2, n // 2) as k:
        for r in range(2):
            emit(k * 2 + r, r, list(range(depth)))
    for step in range(n, n + depth - 1):
        emit(step, step % 2, [s for s in range(depth) if 0 <= step - s < n])


def clear(nc, sems):
    with nc.Block() as block:
        @block.vector
        def _(dve):
            for s in sems:
                dve.sem_clear(s)


def layer0(nc, x, w, z_ext, nb=B):
    qk_split = nc.dram_tensor("qk_split", [2, 2, C, L], F32, kind="Internal").ap()
    with ExitStack() as ctx:
        def sb(name, shape, dt=F32):
            return ctx.enter_context(nc.sbuf_tensor(name, shape, dt))

        names = []

        def sem(name):
            s = ctx.enter_context(nc.semaphore(name))
            names.append(s)
            return s

        ps = ctx.enter_context(nc.psum_tensor("ps", [128, 8, CH], F32))
        w_sb = sb("w_sb", [C, 4, C])
        bias = sb("bias", [C, 5])
        bv_sb = sb("bv_sb", [128, C])
        id_sb = sb("id_sb", [128, 128])
        ones_c = sb("ones_c", [C, C])
        sel_o = sb("sel_o", [128, D])
        sel_d = sb("sel_d", [128, NCH, 128])
        ones_d = sb("ones_d", [128, D])
        denom = sb("denom", [128, CH])
        den_parts = sb("den_parts", [128, CH])
        eps = sb("eps", [128, 1])
        q_st = sb("q_st", [128, 2, L], F32R)
        k_st = sb("k_st", [128, 2, L], F32R)
        v_cur = sb("v_cur", [128, HEADS, NT, D])
        v_next = sb("v_next", [128, HEADS, NT, D])
        exps = sb("exps", [128, 4, 2 * CH])
        heads_out = sb("heads_out", [128, HEADS, L])
        mpart = sb("mpart", [128, NCH, NT])
        mneg = sb("mneg", [128, NT])
        mrow = sb("mrow", [NT, 2, 128], F32R)
        split_buf = sb("split_buf", [128, 2, 2, 2, CH], F32R)

        def work(i):
            if i < 8:
                return exps[:, i // 2, CH * (i % 2):CH * (i % 2) + CH]
            i -= 8
            return split_buf[:, i // 4, i // 2 % 2, i % 2, :].bitcast(F32)

        loaded = sem("loaded")
        made = sem("made")
        zero_ready = sem("zero_ready")

        with nc.Block() as block:
            @block.sync
            def _(sp):
                for i, name in enumerate(("Wq", "Wk", "Wv", "Wo")):
                    sp.dma_start(w_sb[:, i, :], w[name]).then_inc(loaded, 16)
                for i, name in enumerate(("bq", "bk", "bo", "gamma", "beta")):
                    sp.dma_start(bias[:, i:i + 1], w[name].rearrange("(c o) -> c o", o=1)).then_inc(loaded, 16)
                sp.dma_start(bv_sb[:, :], w["bv"].rearrange("(o c) -> o c", o=1).to_broadcast([128, C])).then_inc(loaded, 16)
                sp.dma_start(id_sb[:, :], w["ident"]).then_inc(loaded, 16)
                sp.dma_start(sel_d[:, :, :], w["sel_den"]).then_inc(loaded, 16)
                sp.wait_ge(zero_ready, 1)
                for b in range(B):
                    for at in (0, W + L):
                        sp.dma_start(z_ext[b, :, at:at + W], heads_out[:, 0, 0:W]).then_inc(loaded, 16)
                sp.wait_ge(loaded, 16 * (12 + 2 * B))

            @block.gpsimd
            def _(pool):
                pool.memset(heads_out[:, 0, 0:W], 0.0).then_inc(zero_ready, 1)
                pool.memset(ones_d[:, :], 1.0)
                pool.memset(eps[:, :], LN_EPS)
                pool.memset(ones_c[:, :], 1.0 / C)

            @block.vector
            def _(dve):
                for buf in range(2):
                    nc.vector.memset(k_st[PARTS:128, buf, :].bitcast(F32), 1.0)
                dve.wait_ge(loaded, 16 * (12 + 2 * B))
                for r in range(0, 128, D):
                    nc.vector.tensor_copy(sel_o[r:r + D, :], id_sb[r:r + D, r:r + D])
        clear(nc, names)

        q_proj, x_used, split_ready, split_stored, v_ready, psum_read = [
            sem(n) for n in ("q_proj", "x_used", "split_ready", "split_stored", "v_ready", "psum_read")]
        f_ready = sem("f_ready")
        x_even, x_odd, st_even, st_odd = sem("x_even"), sem("x_odd"), sem("st_even"), sem("st_odd")

        def project(b):
            with nc.Block() as block:
                xc = exps[:, 0, :].rearrange("p (a b) -> p a b", a=2)
                full = lambda r, i: work(2 + 2 * r + i)
                hilo = lambda r, i, part: q_dst[:, r, i, part, :]
                q_dst = split_buf

                @block.sync
                def _(sp):
                    sp.sem_inc(x_used, 2)
                    sp.sem_inc(st_even, 16 * 4)
                    sp.sem_inc(st_odd, 16 * 4)
                    def load(c, r):
                        sp.wait_ge(x_used, c + 1)
                        sp.dma_start(xc[:, r, :], x[b, :, bass.ts(c, CH)]).then_inc((x_even, x_odd)[r], 16)

                    def store(c, r):
                        sp.wait_ge(split_ready, c + 3)
                        for i in range(2):
                            for part in range(2):
                                sp.dma_start(qk_split[i, part, :, bass.ts(c, CH)], hilo(r, i, part).bitcast(F32)
                                             ).then_inc((st_even, st_odd)[r], 16)

                    for r in range(2):
                        load(r, r)
                    with sp.Fori(0, NCH // 2 - 1) as k:
                        for r in range(2):
                            load(k * 2 + 2 + r, r)
                            store(k * 2 + r, r)
                    for r in range(2):
                        store(NCH - 2 + r, r)
                    sp.wait_ge(st_even, 64 * (NCH // 2) + 64)
                    sp.wait_ge(st_odd, 64 * (NCH // 2) + 64)

                @block.tensor
                def _(pe):
                    with pe.Fori(0, NCH // 2) as k:
                        for r in range(2):
                            c = k * 2 + r
                            pe.wait_ge((x_even, x_odd)[r], 16 * k + 16)
                            pe.wait_ge(psum_read, c + 1)
                            pe.wait_ge(v_ready, c + 1)
                            for i in range(2):
                                nc.tensor.matmul(ps[:, 3 * r + i, :], w_sb[:, i, :], xc[:, r, :],
                                                 start=True, stop=True).then_inc(q_proj, 1)
                            for j in range(CH // 128):
                                last = nc.tensor.matmul(ps[:, 3 * r + 2, 128 * j:128 * j + 128],
                                                        xc[:, r, 128 * j:128 * j + 128], w_sb[:, 2, :],
                                                        start=True, stop=True)
                            last.then_inc(x_used, 1)

                @block.scalar
                def _(act):
                    act.sem_inc(psum_read, 2)
                    with act.Fori(0, NCH // 2) as k:
                        for r in range(2):
                            c = k * 2 + r
                            act.wait_ge(split_ready, c + 1)
                            for i in range(2):
                                act.wait_ge(q_proj, c * 2 + i + 1)
                                ins = nc.scalar.activation(full(r, i), ps[:, 3 * r + i, :], ACT.Identity,
                                                           bias=bias[:, i:i + 1])
                                if i == 0:
                                    ins.then_inc(f_ready, 1)
                            ins.then_inc(psum_read, 1)

                @block.vector
                def _(dve):
                    dve.sem_inc(split_ready, 2)
                    dve.sem_inc(v_ready, 2)
                    with dve.Fori(0, NCH // 2) as k:
                        for r in range(2):
                            c = k * 2 + r
                            dve.wait_ge(x_used, c + 3)
                            vt = v_next[:, :, bass.ts(c, CH // 128), :].rearrange("p h t d -> p t h d")
                            nc.vector.tensor_tensor(
                                vt, ps[:, 3 * r + 2, :].rearrange("p (t h d) -> p t h d", t=CH // 128, d=D),
                                bv_sb[:, :].rearrange("p (o h d) -> p o h d", o=1, d=D).to_broadcast([128, CH // 128, HEADS, D]),
                                ALU.add).then_inc(v_ready, 1)
                            dve.wait_ge((st_even, st_odd)[r], 64 * k + 64)
                            dve.wait_ge(psum_read, c + 3)
                            for i in range(2):
                                nc.vector.tensor_copy(hilo(r, i, 0), full(r, i)).then_inc(made, 1)
                            for i in range(2):
                                dve.wait_ge(made, c * 2 + i + 1)
                                last = nc.vector.tensor_tensor(hilo(r, i, 1), full(r, i), hilo(r, i, 0).bitcast(F32), ALU.subtract)
                            last.then_inc(split_ready, 1)

            clear(nc, names)

        k_first, k_rest = sem("k_first"), sem("k_rest")
        q_piece = [sem(f"q_piece{i}") for i in range(NCH)]
        smax_ready, smax_done, sexp_ready, exp_done, av_done, out_read, summed, sum_used, den_read, den_stored = [
            sem(n) for n in ("smax_ready", "smax_done", "sexp_ready", "exp_done", "av_done", "out_read", "summed", "sum_used",
                             "den_read", "den_stored")]
        mneg_ready, mt_ready, mrow_hi, mrow_ready, mrow_stored = [
            sem(n) for n in ("mneg_ready", "mt_ready", "mrow_hi", "mrow_ready", "mrow_stored")]

        def attend(h, nxt):
            MAX_BANK, EXP_BANK, OUT_BANK, DEN_BANK = 0, 3, 6, 7
            buf, nbuf = (h or 0) % 2 if h is not None else None, nxt % 2 if nxt is not None else None

            def over_chunks(e, part, lead=None):
                if lead:
                    lead()
                with e.Fori(0, NCH // 2 - 1) as k:
                    for r in range(2):
                        part(k * 2 + r, r)
                for r in range(2):
                    part(NCH - 2 + r, r)

            def pair_sum(u):
                return split_buf[:, u // 4 % 2, u // 2 % 2, u % 2, :].bitcast(F32)

            def free_from(c, t):
                return c * NT + (t if t > 1 else t + 1)

            with nc.Block() as block:
                @block.sync
                def _(sp):
                    if h is not None:
                        sp.sem_inc(den_stored, 16)
                    if nxt is not None:
                        hd = slice(D * nxt, D * nxt + D)

                        def rows(i, c0, c1, sem_):
                            for n, part in enumerate(((0, 1, 0), (0, 0, 1))[i]):
                                sp.dma_start((q_st, k_st)[i][D * n:D * n + D, nbuf, c0 * CH:c1 * CH].bitcast(F32),
                                             qk_split[i, part, hd, c0 * CH:c1 * CH]).then_inc(sem_, 16)
                        rows(1, 0, 1, k_first)
                        rows(0, 0, 1, q_piece[0])
                        rows(0, 1, 2, q_piece[1])
                        rows(1, 1, NCH, k_rest)
                        for c in range(2, NCH):
                            rows(0, c, c + 1, q_piece[c])
                    if h is not None:
                        for c in range(NCH):
                            sp.wait_ge(den_read, c + 2)
                            row = c * 16 + 4 * h
                            sp.dma_start(denom[row:row + 4, :], den_parts[::D, :]).then_inc(den_stored, 16)
                        sp.wait_ge(den_stored, 16 * NCH + 16)
                    if nxt is not None:
                        sp.wait_ge(mrow_ready, 1)
                        for part in range(2):
                            sp.dma_start(q_st[PARTS + part:PARTS + part + 1, nbuf, :].bitcast(F32), mrow[:, part, :].bitcast(F32)).then_inc(mrow_stored, 16)
                        sp.wait_ge(mrow_stored, 32)

                @block.tensor
                def _(pe):
                    def max_tile(c, r, t):
                        if t % (CH // 128) == 0:
                            pe.wait_ge(q_piece[t // (CH // 128)], 48)
                        if t == 0:
                            pe.wait_ge(k_rest if r else k_first, 48)
                        pe.wait_ge(smax_done, free_from(c, t))
                        nc.tensor.matmul(ps[:, MAX_BANK + t % 3, :], q_st[0:PARTS, nbuf, 128 * t:128 * t + 128],
                                         k_st[0:PARTS, nbuf, bass.ts(c, CH)], start=True, stop=True).then_inc(smax_ready, 1)

                    def exp_tile(c, t):
                        pe.wait_ge(exp_done, free_from(c, t))
                        nc.tensor.matmul(ps[:, EXP_BANK + t % 3, :], k_st[0:SHIFT, buf, 128 * t:128 * t + 128],
                                         q_st[0:SHIFT, buf, bass.ts(c, CH)], start=True, stop=True).then_inc(sexp_ready, 1)

                    def scores(c, r, v):
                        for t in range(4 * v, 4 * v + 4):
                            if nxt is not None:
                                max_tile(c, r, t)
                            if h is not None:
                                exp_tile(c, t)

                    def attn_v(c, r, v):
                        if v == 0:
                            pe.wait_ge(out_read, c + 1)
                        pe.wait_ge(exp_done, c * NT + 4 * v + 6)
                        for i in range(4):
                            ins = nc.tensor.matmul(ps[D * i:D * i + D, OUT_BANK, :], v_cur[:, h, 4 * v + i, :],
                                                   exps[:, (2 * v + i // 2) % 4, CH * (i % 2):CH * (i % 2) + CH],
                                                   start=(v == 0), stop=(v == QUADS - 1))
                            if i % 2:
                                ins.then_inc(av_done, 1)
                        if v % 2:
                            if v == 1:
                                pe.wait_ge(den_read, c + 1)
                            pe.wait_ge(summed, c * PAIRS + 2 * v + 10)
                            for j in range(4):
                                u = 2 * v - 2 + j
                                nc.tensor.matmul(ps[D * j:D * j + D, DEN_BANK, :], ones_d[:, :], pair_sum(u),
                                                 start=(v == 1), stop=(v == QUADS - 1)).then_inc(sum_used, 1)

                    def part(c, r):
                        for v in range(QUADS):
                            if v + 1 < QUADS:
                                scores(c, r, v + 1)
                            elif not isinstance(c, int) or c + 1 < NCH:
                                scores(c + 1, 1 - r, 0)
                            if h is not None:
                                attn_v(c, r, v)

                    over_chunks(pe, part, lambda: scores(0, 0, 0))
                    if nxt is not None:
                        pe.wait_ge(mneg_ready, 1)
                        nc.tensor.transpose(ps[0:NT, 0, 0:128], mneg[:, :], id_sb[:, :]).then_inc(mt_ready, 1)

                @block.scalar
                def _(act):
                    if h is None:
                        return
                    act.sem_inc(exp_done, 2)
                    act.sem_inc(out_read, 1)

                    def read_out(c):
                        act.wait_ge(av_done, c * PAIRS + PAIRS + 4)
                        nc.scalar.copy(heads_out[:, h, bass.ts(c, CH)], ps[:, OUT_BANK, :]).then_inc(out_read, 1)

                    def part(c, r):
                        for t in range(NT):
                            act.wait_ge(sexp_ready, c * NT + t + 1)
                            u, half = t // 2, t % 2
                            if half == 0:
                                act.wait_ge(av_done, c * PAIRS + u + 1)
                                act.wait_ge(summed, c * PAIRS + u + 5)
                            nc.scalar.activation(exps[:, u % 4, CH * half:CH * half + CH], ps[:, EXP_BANK + t % 3, :],
                                                 ACT.Exp, scale=SCALE).then_inc(exp_done, 1)
                            if t == 3 and (not isinstance(c, int) or c > 0):
                                read_out(c - 1)

                    part(0, 0)
                    with act.Fori(0, NCH // 2 - 1) as k:
                        for r in range(2):
                            part(k * 2 + r + 1, 1 - r)
                    part(NCH - 1, 1)
                    read_out(NCH - 1)

                @block.gpsimd
                def _(pool):
                    if h is None:
                        return
                    pool.sem_inc(av_done, 4)
                    pool.sem_inc(summed, 8)
                    pool.sem_inc(sum_used, 8)
                    with pool.Fori(0, NCH) as c:
                        for u in range(PAIRS):
                            pool.wait_ge(exp_done, c * NT + 2 * u + 4)
                            pool.wait_ge(sum_used, c * PAIRS + u + 1)
                            pool.tensor_tensor(pair_sum(u), exps[:, u % 4, 0:CH], exps[:, u % 4, CH:2 * CH], ALU.add).then_inc(summed, 1)

                @block.vector
                def _(dve):
                    if nxt is not None:
                        dve.sem_inc(smax_done, 2)
                    if h is not None:
                        dve.sem_inc(den_read, 1)

                    def read_den(c):
                        dve.wait_ge(sum_used, c * PAIRS + PAIRS + 8)
                        dve.wait_ge(den_stored, c * 16 + 16)
                        nc.vector.tensor_copy(den_parts[:, :], ps[:, DEN_BANK, :]).then_inc(den_read, 1)

                    def part(c, r):
                        for t in range(NT):
                            if nxt is not None:
                                dve.wait_ge(smax_ready, c * NT + t + 1)
                                nc.vector.tensor_reduce(mpart[:, c, t:t + 1], ps[:, MAX_BANK + t % 3, :], AX.X, ALU.max).then_inc(smax_done, 1)
                            if t == 3 and h is not None and (not isinstance(c, int) or c > 0):
                                read_den(c - 1)

                    part(0, 0)
                    with dve.Fori(0, NCH // 2 - 1) as k:
                        for r in range(2):
                            part(k * 2 + r + 1, 1 - r)
                    part(NCH - 1, 1)
                    if h is not None:
                        read_den(NCH - 1)
                    if nxt is None:
                        return
                    dve.wait_ge(smax_done, NCH * NT + 2)
                    nc.vector.tensor_reduce(mneg[:, :], mpart[:, :, :].rearrange("p c t -> p t c"), AX.X, ALU.max,
                                            negate=True).then_inc(mneg_ready, 1)
                    dve.wait_ge(mt_ready, 1)
                    nc.vector.tensor_copy(mrow[:, 0, :], ps[0:NT, 0, 0:128]).then_inc(mrow_hi, 1)
                    dve.wait_ge(mrow_hi, 1)
                    nc.vector.tensor_tensor(mrow[:, 1, :], ps[0:NT, 0, 0:128], mrow[:, 0, :].bitcast(F32), ALU.subtract).then_inc(mrow_ready, 1)
            clear(nc, names)

        def take_v():
            with nc.Block() as block:
                @block.vector
                def _(dve):
                    nc.vector.tensor_copy(v_cur[:, :, :, :], v_next[:, :, :, :])

        (od_ready, log_d, recip_d, normed, wo_ready, y_ready, mean_ready, centred, squared, var_ready, log_v, rstd_ready,
         scaled, z_ready, z_stored) = [sem(n) for n in (
             "od_ready", "log_d", "recip_d", "normed", "wo_ready", "y_ready", "mean_ready", "centred", "squared", "var_ready", "log_v",
             "rstd_ready", "scaled", "z_ready", "z_stored")]

        def finish(b):
            X_IN, RECIP, NORMED, Y, CENTRED, SQUARE, RSTD = range(7)
            buf = lambda what, r: work(2 * what + r)
            Z, SCALED = range(2)
            with nc.Block() as block:
                @block.sync
                def _(sp):
                    sp.sem_inc(y_ready, 2)
                    with sp.Fori(0, NCH // 2) as k:
                        for r in range(2):
                            c = k * 2 + r
                            sp.wait_ge(y_ready, c + 1)
                            sp.dma_start(buf(X_IN, r), x[b, :, bass.ts(c, CH)]).then_inc((x_even, x_odd)[r], 16)
                    for i in range(2):
                        sp.wait_ge(z_ready, (NCH // 2, NCH)[i])
                        sp.dma_start(z_ext[b, :, W + i * L // 2:W + (i + 1) * L // 2], heads_out[:, Z, i * L // 2:(i + 1) * L // 2]
                                     ).then_inc(z_stored, 16)
                    sp.wait_ge(z_stored, 32)

                @block.tensor
                def _(pe):
                    for step in range(NCH + 3):
                        c = step
                        if c < NCH:
                            pe.wait_ge(normed, c + 1)
                            nc.tensor.matmul(ps[:, 1, :], sel_d[:, c, :], denom[:, :], start=True, stop=True)
                            for h in range(HEADS):
                                ins = nc.tensor.matmul(ps[D * h:D * h + D, 0, :], sel_o[:, :],
                                                       heads_out[:, h, c * CH:c * CH + CH], start=True, stop=True)
                            ins.then_inc(od_ready, 1)
                        c, r = step - 1, (step - 1) % 2
                        if 0 <= c < NCH:
                            pe.wait_ge(normed, c + 2)
                            pe.wait_ge(y_ready, c + 1)
                            nc.tensor.matmul(ps[:, 2 + r, :], w_sb[:, 3, :], buf(NORMED, r), start=True, stop=True).then_inc(wo_ready, 1)
                        c, r = step - 2, step % 2
                        if 0 <= c < NCH:
                            pe.wait_ge(y_ready, c + 3)
                            pe.wait_ge(centred, c + 1)
                            nc.tensor.matmul(ps[:, 4 + r, :], ones_c[:, :], buf(Y, r), start=True, stop=True).then_inc(mean_ready, 1)
                        c, r = step - 3, (step - 3) % 2
                        if 0 <= c < NCH:
                            pe.wait_ge(squared, c + 1)
                            pe.wait_ge(rstd_ready, c + 1)
                            nc.tensor.matmul(ps[:, 6 + r, :], ones_c[:, :], buf(SQUARE, r), start=True, stop=True).then_inc(var_ready, 1)

                @block.scalar
                def _(act):
                    act.sem_inc(rstd_ready, 2)
                    nc.scalar.preload_act_table_set(LN_EXP)

                    def emit(step, par, stages):
                        if 0 in stages:
                            c, r = step, par
                            act.wait_ge(od_ready, c + 1)
                            act.wait_ge(normed, c + 1)
                            nc.scalar.activation(buf(RECIP, r), ps[:, 1, :], ACT.Ln).then_inc(log_d, 1)
                            act.wait_ge(log_d, c + 1)
                            nc.scalar.activation(buf(RECIP, r), buf(RECIP, r), ACT.Exp, scale=-1.0).then_inc(recip_d, 1)
                        if 2 in stages:
                            c, r = step - 2, par
                            act.wait_ge(centred, c + 3)
                            nc.scalar.activation(buf(SQUARE, r), buf(CENTRED, r), ACT.Square).then_inc(squared, 1)
                        if 3 in stages:
                            c, r = step - 3, (par - 3) % 2
                            act.wait_ge(var_ready, c + 1)
                            act.wait_ge(scaled, c + 1)
                            nc.scalar.activation(buf(RSTD, r), ps[:, 6 + r, :], ACT.Ln, bias=eps[:, 0:1]).then_inc(log_v, 1)
                            act.wait_ge(log_v, c + 1)
                            nc.scalar.activation(buf(RSTD, r), buf(RSTD, r), ACT.Exp, scale=-0.5).then_inc(rstd_ready, 1)
                        if 4 in stages:
                            c = step - 4
                            act.wait_ge(scaled, c + 3)
                            nc.scalar.activation(heads_out[:, Z, bass.ts(c, CH)], heads_out[:, SCALED, bass.ts(c, CH)], ACT.Identity,
                                                 bias=bias[:, 4:5], scale=bias[:, 3:4]).then_inc(z_ready, 1)
                    pipelined(act, NCH, 5, emit)

                @block.vector
                def _(dve):
                    dve.sem_inc(normed, 1)
                    dve.sem_inc(centred, 2)
                    dve.sem_inc(scaled, 2)

                    def emit(step, par, stages):
                        if 0 in stages:
                            c, r = step, par
                            dve.wait_ge(recip_d, c + 1)
                            nc.vector.tensor_tensor(buf(NORMED, r), ps[:, 0, :], buf(RECIP, r), ALU.mult).then_inc(normed, 1)
                        if 1 in stages:
                            c, r = step - 1, (par - 1) % 2
                            dve.wait_ge((x_even, x_odd)[r], (c - r) * 8 + 16)
                            dve.wait_ge(wo_ready, c + 1)
                            nc.vector.scalar_tensor_tensor(buf(Y, r), ps[:, 2 + r, :], bias[:, 2:3], buf(X_IN, r), ALU.add, ALU.add
                                                           ).then_inc(y_ready, 1)
                        if 2 in stages:
                            c, r = step - 2, par
                            dve.wait_ge(mean_ready, c + 1)
                            dve.wait_ge(scaled, c + 1)
                            nc.vector.tensor_tensor(buf(CENTRED, r), buf(Y, r), ps[:, 4 + r, :], ALU.subtract).then_inc(centred, 1)
                        if 3 in stages:
                            c, r = step - 3, (par - 3) % 2
                            dve.wait_ge(rstd_ready, c + 3)
                            nc.vector.tensor_tensor(heads_out[:, SCALED, bass.ts(c, CH)], buf(CENTRED, r), buf(RSTD, r), ALU.mult
                                                    ).then_inc(scaled, 1)
                    pipelined(dve, NCH, 4, emit)
            clear(nc, names)

        def batch(b, last):
            take_v()
            for h in range(HEADS):
                if h == HEADS - 1:
                    if not last:
                        project(b + 1)
                    attend(h, None if last else 0)
                else:
                    attend(h, h + 1)
            finish(b)

        project(0)
        attend(None, 0)
        if nb > 1:
            with nc.Fori(0, nb - 1) as b:
                batch(b, False)
        batch(nb - 1, True)


def denominators():
    m = np.zeros((128, NCH, HEADS, D), np.float32)
    for c in range(NCH):
        for h in range(HEADS):
            m[16 * c + 4 * h:16 * c + 4 * h + 4, c, h] = 1
    return m.reshape(128, NCH, 128)


ST = 16
GC = 128 // ST
INNER = 2 * C
LN_EXP = "natural_log_exp_and_others"
LC = 512
STEPS = L // LC
ROWS = LC // W
HALO = (ROWS + 2) * W
GROUPS = INNER // GC
RANK = 8


def layer1(nc, z_ext, w, out, nb=B):
    NIT = nb * STEPS
    with ExitStack() as ctx:
        def sb(name, shape, dt=F32):
            return ctx.enter_context(nc.sbuf_tensor(name, shape, dt))

        names = []

        def sem(name):
            s = ctx.enter_context(nc.semaphore(name))
            names.append(s)
            return s

        ps = ctx.enter_context(nc.psum_tensor("ps1", [128, 8, CH], F32))
        DT_BANK, U_BANK, Y_BANK, O_BANK, ITEM_BANK = 0, 2, 4, 5, 6
        win = sb("win", [C, 2 * INNER])
        wtap = sb("wtap", [C, 4, INNER])
        wxd = sb("wxd", [128, 2, 128])
        wdt = sb("wdt", [128, INNER])
        sel_b = sb("sel_b", [128, 128])
        sel_c = sb("sel_c", [128, 128])
        sel_g = sb("sel_g", [128, 8, 128], F32R)
        sel_y = sb("sel_y", [128, 4, 32])
        wconv = sb("wconv", [C, 9, C])
        wspec = sb("wspec", [C, 4, C])
        wmix = sb("wmix", [C, 4, C])
        hilb = sb("hilb", [128, 128])
        wout = sb("wout", [128, 2, C])
        cols = sb("cols", [128, 9])
        a_neg = sb("a_neg", [128, GROUPS])
        carry = sb("carry", [128, STEPS + 1, GROUPS])
        row0 = sb("row0", [128, STEPS, W])
        hil0 = sb("hil0", [128, W])
        za = sb("za", [128, 2, HALO])
        zp = sb("zp", [128, 2, ROWS + 2, W + 2])
        zj = sb("zj", [128, 2, LC])
        xs = sb("xs", [128, 2, 2, LC])
        gz = sb("gz", [128, 2, 2, LC])
        s_dt = sb("s_dt", [128, 2, 4, LC], F32R)
        s_u = sb("s_u", [128, 2, 4, LC], F32R)
        b_rep = sb("b_rep", [128, 2, LC])
        c_rep = sb("c_rep", [128, 2, LC])
        g_t = sb("g_t", [128, 2, LC])
        o_sb = sb("o_sb", [128, 2, LC])
        stage_j = sb("stage_j", [128, ROWS, W])
        edt = sb("edt", [128, 2, LC])
        dt = sb("dt", [128, 2, LC])
        ux = sb("ux", [128, 2, LC])
        xd = sb("xd", [128, LC])
        yt = sb("yt", [128, 2, LC])
        NDA, NBU, NHH, NHC = 8, 4, 8, 8
        d_a = sb("d_a", [128, NDA, LC])
        b_u = sb("b_u", [128, NBU, LC])
        hh = sb("hh", [128, NHH, LC])
        hc = sb("hc", [128, NHC, LC])

        loaded, mixed, a_exp, carry_zero, row_zero, halved = [sem(n) for n in (
            "loaded1", "mixed", "a_exp", "carry_zero", "row_zero", "halved")]
        NLOAD = 15 * 16
        with nc.Block() as block:
            @block.sync
            def _(sp):
                for dst, src in (
                        (win[:, :], w["win"]), (xs[:, :, :, :].rearrange("p a b c -> p (a b c)")[:, 0:4 * INNER],
                                                w["taps"].rearrange("(o k) e -> o (k e)", o=1).to_broadcast([C, 4 * INNER])),
                        (wxd[:, :, :], w["wxd"]), (wdt[:, :], w["wdt"]), (sel_b[:, :], w["sel_b"]), (sel_c[:, :], w["sel_c"]),
                        (hh[:, 0:2, :].rearrange("p a b -> p (a b)"), w["sel_g"]), (sel_y[:, :, :], w["sel_y"]),
                        (wconv[:, :, :], w["wconv"]), (wspec[:, :, :], w["wspec"]), (hilb[:, :], w["hilb"]),
                        (hil0[:, :], w["hil0"].to_broadcast([128, W])), (wout[:, :, :], w["wout"]), (cols[:, :], w["cols"]),
                        (a_neg[:, :], w["a_log"])):
                    sp.dma_start(dst, src).then_inc(loaded, 16)
                sp.wait_ge(loaded, NLOAD)

            @block.gpsimd
            def _(pool):
                pool.memset(zp[:, :, :, :], 0.0)
                pool.memset(carry[:, :, :], 0.0)
                pool.memset(row0[:, :, :], 0.0).then_inc(row_zero, 1)

            @block.scalar
            def _(act):
                act.wait_ge(loaded, NLOAD)
                nc.scalar.activation(a_neg[:, :], a_neg[:, :], ACT.Exp).then_inc(a_exp, 1)
                act.wait_ge(a_exp, 1)
                nc.scalar.mul(a_neg[:, :], a_neg[:, :], -1.0)

            @block.vector
            def _(dve):
                dve.wait_ge(loaded, NLOAD)
                nc.vector.tensor_copy(sel_g[:, :, :].rearrange("p a b -> p (a b)"), hh[:, 0:2, :].rearrange("p a b -> p (a b)"))
                nc.vector.tensor_tensor(wtap[:, :, :],
                                        xs[:, :, :, :].rearrange("p a b c -> p (a b c)")[:, 0:4 * INNER].rearrange("p (k e) -> p k e", k=4),
                                        win[:, 0:INNER].rearrange("p (o e) -> p o e", o=1).to_broadcast([C, 4, INNER]), ALU.mult)
                RR, RI, IR, II = range(4)
                nc.vector.tensor_tensor(wmix[:, 0, :], wspec[:, RR, :], wspec[:, II, :], ALU.add)
                nc.vector.tensor_tensor(wmix[:, 1, :], wspec[:, RR, :], wspec[:, II, :], ALU.subtract)
                nc.vector.tensor_tensor(wmix[:, 2, :], wspec[:, IR, :], wspec[:, RI, :], ALU.subtract)
                nc.vector.tensor_tensor(wmix[:, 3, :], wspec[:, IR, :], wspec[:, RI, :], ALU.add).then_inc(mixed, 1)
                dve.wait_ge(mixed, 1)
                nc.vector.tensor_scalar_mul(wmix[:, :, :], wmix[:, :, :], 0.5).then_inc(halved, 1)
                dve.wait_ge(row_zero, 1)
                nc.vector.tensor_scalar(row0[:, 0, :], hil0[:, :], cols[:, 8:9], None, ALU.mult).then_inc(halved, 1)
                dve.wait_ge(halved, 2)
                nc.vector.tensor_tensor(wconv[:, 4, :], wconv[:, 4, :], wmix[:, 0, :], ALU.add)
                nc.vector.tensor_tensor(row0[:, 0, 0:1], row0[:, 0, 0:1], cols[:, 7:8], ALU.add)
        clear(nc, names)

        (z_in, flipped, item, item_read, sp_log, dt_sum, u_prod, hi_ready, lo_ready,
         dt_rep, u_rep, da_ready, bu_ready, scanned, kept, hc_ready, y_done, y_added, gated, z_used, o_ready, o_copied,
         o_full, o_even, o_odd) = [sem(x) for x in (
             "z_in", "flipped", "item", "item_read", "sp_log", "dt_sum", "u_prod",
             "hi_ready", "lo_ready", "dt_rep", "u_rep", "da_ready", "bu_ready", "scanned", "kept", "hc_ready", "y_done",
             "y_added", "gated", "z_used", "o_ready", "o_copied", "o_full", "o_even", "o_odd")]

        XS, XD, DT, BI, CI, GATE, GI, NITEM = 0, 2, 3, 5, 6, 7, 9, 10
        G = GROUPS
        LEAD = 4

        def ge(e, s, value):
            if not isinstance(value, int) or value > 0:
                e.wait_ge(s, value)

        def column(g):
            half, jj, i = g // 16, g // 4 % 4, g % 4
            return 2 * half + i // 2, jj + 4 * (i % 2)

        def steps(e, prepare, emit, tail):
            for g in range(G):
                prepare(0, 0, g)
            for it in range(2):
                emit(it, it)
            with e.Fori(1, NIT // 2) as k:
                for r in range(2):
                    emit(k * 2 + r, r)
            tail()

        with nc.Block() as block:
            @block.sync
            def _(sp):
                def load(j, p):
                    jw = j if isinstance(j, int) else j % NIT
                    b, lc = jw // STEPS, jw % STEPS
                    ge(sp, z_used, j - 1)
                    ge(sp, flipped, 2 * j)
                    sp.dma_start(za[:, p, :], z_ext[b, :, bass.ds(lc * LC, HALO)]).then_inc(z_in, 16)
                    sp.dma_start(zp[:, p, :, 1:W + 1], z_ext[b, :, bass.ds(lc * LC, HALO)].rearrange("c (h w) -> c h w", w=W)).then_inc(z_in, 16)
                    last = (STEPS - 1 - lc) * LC + W
                    sp.dma_start(stage_j[:, 0:ROWS - 1, :], z_ext[b, :, bass.ds(last + W, LC - W)].rearrange("c (h w) -> c h w", w=W)).then_inc(z_in, 16)
                    sp.dma_start(stage_j[:, ROWS - 1, :], z_ext[b, :, bass.ds((STEPS - lc) % STEPS * LC + W, W)]).then_inc(z_in, 16)

                def store(j, p):
                    b, lc = j // STEPS, j % STEPS
                    sp.wait_ge(o_full, j + 1)
                    sp.dma_start(out[b, :, bass.ds(lc * LC, LC)], o_sb[:, p, :]).then_inc((o_even, o_odd)[p], 16)

                load(0, 0)
                load(1, 1)
                load(2, 0)
                with sp.Fori(1, NIT // 2) as k:
                    store(k * 2 - 2, 0)
                    load(k * 2 + 1, 1)
                    store(k * 2 - 1, 1)
                    load(k * 2 + 2, 0)
                store(NIT - 2, 0)
                store(NIT - 1, 1)
                sp.wait_ge(o_even, 16 * (NIT // 2))
                sp.wait_ge(o_odd, 16 * (NIT // 2))
                sp.wait_ge(z_in, 64 * (NIT + 1))

            @block.tensor
            def _(pe):
                def bank(n):
                    return ps[:, ITEM_BANK + n % 2, :]

                def begin(j, n):
                    ge(pe, item_read, j * NITEM + n - 1)

                def prepare(j, p, g):
                    if 1 <= g <= 7:
                        if g == 1:
                            pe.wait_ge(z_in, j * 64 + 64)
                        for n in (g - 1,) if g < 7 else (6, 7):
                            h, k = n // 4, n % 4
                            if k == 0:
                                begin(j, XS + h)
                            ins = nc.tensor.matmul(bank(XS + h), wtap[:, k, 128 * h:128 * h + 128],
                                                   za[:, p, W - 3 + k:W - 3 + k + LC], start=(k == 0), stop=(k == 3))
                            if k == 3:
                                ins.then_inc(item, 1)
                    elif g in (11, 12):
                        i = g - 11
                        if i == 0:
                            begin(j, XD)
                            pe.wait_ge(item_read, j * NITEM + XS + 2)
                        ins = nc.tensor.matmul(bank(XD), wxd[:, i, :], xs[:, p, i, :], start=(i == 0), stop=(i == 1))
                        if i == 1:
                            ins.then_inc(item, 1)
                    elif g in (15, 16):
                        n = DT + g - 15
                        begin(j, n)
                        pe.wait_ge(item_read, j * NITEM + XD + 1)
                        nc.tensor.matmul(bank(n), wdt[:, 128 * (g - 15):128 * (g - 15) + 128], xd[:, :], start=True, stop=True
                                         ).then_inc(item, 1)
                    elif g in (19, 20):
                        n = BI + g - 19
                        begin(j, n)
                        nc.tensor.matmul(bank(n), (sel_b, sel_c)[g - 19][:, :], xd[:, :], start=True, stop=True).then_inc(item, 1)
                    elif g in (22, 23):
                        n, h = GATE + g - 22, g - 22
                        begin(j, n)
                        nc.tensor.matmul(bank(n), win[:, INNER + 128 * h:INNER + 128 * h + 128], za[:, p, W:W + LC],
                                         start=True, stop=True).then_inc(item, 1)
                    elif g == 29:
                        begin(j, GI)
                        pe.wait_ge(flipped, j * 2 + 2)
                        for i in range(LC // 128):
                            o = bank(GI)[:, 128 * i:128 * i + 128]
                            nc.tensor.matmul(o, za[:, p, W + 128 * i:W + 128 * i + 128], wmix[:, 2, :], start=True, stop=False)
                            ins = nc.tensor.matmul(o, zj[:, p, 128 * i:128 * i + 128], wmix[:, 3, :], start=False, stop=True)
                        ins.then_inc(item, 1)

                def fill(it, p, n):
                    o = ps[:, O_BANK, :]
                    if n < 9:
                        if n == 0:
                            ge(pe, o_copied, it)
                        dy, dx = n // 3, n % 3
                        nc.tensor.matmul(o.rearrange("p (a b) -> p a b", b=W), wconv[:, n, :], zp[:, p, dy:dy + ROWS, dx:dx + W],
                                         start=(n == 0), stop=False)
                    else:
                        nc.tensor.matmul(o, wmix[:, 1, :], zj[:, p, :], start=False, stop=False).then_inc(z_used, 1)

                def fill_g(it, p):
                    for i in range(LC // 128):
                        nc.tensor.matmul(ps[:, O_BANK, 128 * i:128 * i + 128], g_t[:, p, 128 * i:128 * i + 128], hilb[:, :],
                                         start=False, stop=False)

                def sum_states(it, n):
                    pe.wait_ge(hc_ready, it * G + 4 * n + 4)
                    if n % 4 == 0:
                        ge(pe, y_added, it * 2 + n // 4)
                    for i in range(4):
                        ins = nc.tensor.matmul(ps[32 * i:32 * i + 32, Y_BANK, :], sel_y[:, n % 4, :], hc[:, (4 * n + i) % NHC, :],
                                               start=(n % 4 == 0), stop=(n % 4 == 3))
                    ins.then_inc(y_done, 1)

                def out_proj(it, i):
                    if i == 0:
                        pe.wait_ge(gated, it * 2 + 2)
                    ins = nc.tensor.matmul(ps[:, O_BANK, :], wout[:, i, :], yt[:, i, :], start=False, stop=(i == 1))
                    if i == 1:
                        ins.then_inc(o_ready, 1)

                def repeat_dt(it, p, g):
                    s, j = column(g)
                    if g == 0:
                        pe.wait_ge(lo_ready, it * 4 + 2)
                    ge(pe, da_ready, it * G + g - 1)
                    nc.tensor.matmul(ps[:, DT_BANK + g % 2, :], sel_g[:, j, :], s_dt[:, p, s, :], start=True, stop=True).then_inc(dt_rep, 1)

                def repeat_u(it, p, g):
                    s, j = column(g)
                    if g == 0:
                        pe.wait_ge(lo_ready, it * 4 + 4)
                    ge(pe, bu_ready, it * G + g - 1)
                    nc.tensor.matmul(ps[:, U_BANK + g % 2, :], sel_g[:, j, :], s_u[:, p, s, :], start=True, stop=True).then_inc(u_rep, 1)

                FILLS = (18, 21, 21, 24, 24, 25, 26, 27, 27, 28)

                def emit(it, p):
                    for g in range(G):
                        if isinstance(it, int) and it == g == 0:
                            for d in range(LEAD):
                                repeat_dt(it, p, d)
                        repeat_u(it, p, g)
                        prepare(it + 1, 1 - p, g)
                        if g in (0, 4) and not (isinstance(it, int) and it == 0):
                            sum_states(it - 1, 6 + g // 4)
                        if g in (13, 14) and not (isinstance(it, int) and it == 0):
                            out_proj(it - 1, g - 13)
                        for n in range(10):
                            if FILLS[n] == g:
                                fill(it, p, n)
                        if g == 30:
                            fill_g(it, p)
                        if g >= 8 and g % 4 == 0:
                            sum_states(it, g // 4 - 2)
                        if g + LEAD < G:
                            repeat_dt(it, p, g + LEAD)
                        else:
                            repeat_dt(it + 1, 1 - p, g + LEAD - G)

                def tail():
                    sum_states(NIT - 1, 6)
                    sum_states(NIT - 1, 7)
                    for i in range(2):
                        out_proj(NIT - 1, i)
                steps(pe, prepare, emit, tail)

            @block.scalar
            def _(act):
                def take(j, n):
                    act.wait_ge(item, j * NITEM + n + 1)
                    return ps[:, ITEM_BANK + n % 2, :]

                def silus(dst, j, n, bias):
                    for h in range(2):
                        nc.scalar.activation(dst[:, h, :], take(j, n + h), ACT.Silu, bias=bias(h)).then_inc(item_read, 1)
                    nc.scalar.preload_act_table_set(LN_EXP)

                def high(j, p, stack, src, part):
                    a = slice(64 * part, 64 * part + 64)
                    nc.scalar.copy(stack[a, p, part::2, :], src[a, :, :]).then_inc(hi_ready, 1)

                def prepare(j, p, g):
                    if g == 3:
                        act.wait_ge(z_in, j * 64 + 64)
                        zf = zj[:, p, :].rearrange("p (h w) -> p h w", w=W)
                        nc.scalar.copy(zf[:, :, 0:1], stage_j[:, ::-1, 0:1]).then_inc(flipped, 1)
                        nc.scalar.copy(zf[:, :, 1:W], stage_j[:, ::-1, W - 1:0:-1]).then_inc(flipped, 1)
                    elif g == 10:
                        ge(act, y_added, j * 2 - 2)
                        silus(xs[:, p, :, :], j, XS, lambda h: cols[:, h:h + 1])
                    elif g == 15:
                        nc.scalar.copy(xd[:, :], take(j, XD)).then_inc(item_read, 1)
                    elif g in (19, 20):
                        h = g - 19
                        if h == 0:
                            ge(act, lo_ready, j * 4)
                        nc.scalar.activation(dt[:, h, :], take(j, DT + h), ACT.Relu, bias=cols[:, 2 + h:3 + h])
                        nc.scalar.activation(edt[:, h, :], take(j, DT + h), ACT.Abs, bias=cols[:, 2 + h:3 + h]).then_inc(item_read, 1)
                    elif g == 21:
                        act.wait_ge(item_read, j * NITEM + DT + 2)
                        nc.scalar.activation(edt[:, :, :], edt[:, :, :], ACT.Exp, scale=-1.0).then_inc(sp_log, 1)
                    elif g == 22:
                        act.wait_ge(sp_log, j * 2 + 1)
                        nc.scalar.activation(edt[:, :, :], edt[:, :, :], ACT.Ln, bias=1.0).then_inc(sp_log, 1)
                    elif g in (23, 24):
                        nc.scalar.copy((b_rep, c_rep)[g - 23][:, p, :], take(j, BI + g - 23)).then_inc(item_read, 1)
                    elif g in (25, 26):
                        act.wait_ge(dt_sum, j + 1)
                        high(j, p, s_dt, dt, g - 25)
                    elif g in (27, 28):
                        act.wait_ge(u_prod, j + 1)
                        high(j, p, s_u, ux, g - 27)
                    elif g == 29:
                        ge(act, gated, j * 2 - 2)
                        silus(gz[:, p, :, :], j, GATE, lambda h: 0.0)
                    elif g == 31:
                        nc.scalar.copy(g_t[:, p, :], take(j, GI)).then_inc(item_read, 1)

                KEEP = 5

                def last_state(it, p, g):
                    act.wait_ge(scanned, it * G + g + 1)
                    s, j = column(g)
                    nc.scalar.copy(carry[:, it % STEPS + 1, s * 8 + j:s * 8 + j + 1],
                                   hh[:, g % NHH, LC - 1:LC]).then_inc(kept, 1)

                def decay(it, g):
                    s, j = column(g)
                    act.wait_ge(dt_rep, it * G + g + 1)
                    ge(act, scanned, it * G + g - NDA + 1)
                    nc.scalar.activation(d_a[:, g % NDA, :], ps[:, DT_BANK + g % 2, :], ACT.Exp,
                                         scale=a_neg[:, s * 8 + j:s * 8 + j + 1]).then_inc(da_ready, 1)

                def emit(it, p):
                    for g in range(G):
                        decay(it, g)
                        if g >= KEEP:
                            last_state(it, p, g - KEEP)
                        elif not (isinstance(it, int) and it == 0):
                            last_state(it - 1, 1 - p, G + g - KEEP)
                        prepare(it + 1, 1 - p, g)
                        if g == 17 and not (isinstance(it, int) and it == 0):
                            output(it - 1, 1 - p)

                def output(it, p):
                    act.wait_ge(o_ready, it + 1)
                    if not (isinstance(it, int) and it < 2):
                        act.wait_ge((o_even, o_odd)[p], (it - p) * 8)
                    nc.scalar.activation(o_sb[:, p, :], ps[:, O_BANK, :], ACT.Identity, bias=cols[:, 6:7]).then_inc(o_copied, 1)

                def tail():
                    for g in range(LEAD - 2):
                        decay(NIT, g)
                    for g in range(G - KEEP, G):
                        last_state(NIT - 1, 1, g)
                    output(NIT - 1, 1)
                nc.scalar.preload_act_table_set(LN_EXP)
                steps(act, prepare, emit, tail)

            @block.vector
            def _(dve):
                def low(j, p, stack, src, part, n):
                    a, b = slice(64 * part, 64 * part + 64), slice(64 - 64 * part, 128 - 64 * part)
                    dve.wait_ge(hi_ready, j * 4 + 2 * n + part + 1)
                    nc.vector.tensor_tensor(stack[b, p, part::2, :], src[a, :, :], stack[a, p, part::2, :].bitcast(F32), ALU.subtract
                                            ).then_inc(lo_ready, 1)

                def prepare(j, p, g):
                    if g == 20:
                        dve.wait_ge(sp_log, j * 2 + 2)
                        nc.vector.tensor_tensor(dt[:, :, :], dt[:, :, :], edt[:, :, :], ALU.add).then_inc(dt_sum, 1)
                    elif g == 21:
                        dve.wait_ge(dt_sum, j + 1)
                        nc.vector.tensor_tensor(ux[:, :, :], dt[:, :, :], xs[:, p, :, :], ALU.mult).then_inc(u_prod, 1)
                    elif g in (25, 26):
                        low(j, p, s_dt, dt, g - 25, 0)
                    elif g in (27, 28):
                        low(j, p, s_u, ux, g - 27, 1)

                def add_skip(it, p, half):
                    dve.wait_ge(y_done, it * 8 + 4 * half + 4)
                    ge(dve, o_ready, it)
                    nc.vector.scalar_tensor_tensor(yt[:, half, :], xs[:, p, half, :], cols[:, 4 + half:5 + half], ps[:, Y_BANK, :],
                                                   ALU.mult, ALU.add).then_inc(y_added, 1)

                def add_row(it, p):
                    dve.wait_ge(o_copied, it + 1)
                    nc.vector.tensor_tensor(o_sb[:, p, 0:W], o_sb[:, p, 0:W], row0[:, it % STEPS, :], ALU.add).then_inc(o_full, 1)

                def times_b(it, p, g):
                    dve.wait_ge(u_rep, it * G + g + 1)
                    if g == 0:
                        dve.wait_ge(item_read, it * NITEM + BI + 1)
                    ge(dve, scanned, it * G + g - NBU + 1)
                    nc.vector.tensor_tensor(b_u[:, g % NBU, :], ps[:, U_BANK + g % 2, :], b_rep[:, p, :], ALU.mult).then_inc(bu_ready, 1)

                def emit(it, p):
                    times_b(it, p, 0)
                    for g in range(G):
                        if g + 1 < G:
                            times_b(it, p, g + 1)
                        s, j = column(g)
                        dve.wait_ge(bu_ready, it * G + g + 1)
                        dve.wait_ge(da_ready, it * G + g + 1)
                        ge(dve, hc_ready, it * G + g - NHH + 1)
                        ge(dve, kept, it * G + g - NHH + 1)
                        nc.vector.tensor_tensor_scan(hh[:, g % NHH, :], d_a[:, g % NDA, :], b_u[:, g % NBU, :],
                                                     carry[:, it % STEPS, s * 8 + j:s * 8 + j + 1], ALU.mult, ALU.add).then_inc(scanned, 1)
                        prepare(it + 1, 1 - p, g)
                        if g == 21:
                            add_skip(it, p, 0)
                        if not (isinstance(it, int) and it == 0):
                            if g == 5:
                                add_skip(it - 1, 1 - p, 1)
                            if g == 16:
                                add_row(it - 1, 1 - p)

                def tail():
                    add_skip(NIT - 1, 1, 1)
                    add_row(NIT - 1, 1)
                steps(dve, prepare, emit, tail)

            @block.gpsimd
            def _(pool):
                def prepare(j, p, g):
                    pass

                def gate(it, p, half):
                    pool.wait_ge(y_added, it * 2 + half + 1)
                    pool.tensor_tensor(yt[:, half, :], yt[:, half, :], gz[:, p, half, :], ALU.mult).then_inc(gated, 1)

                def emit(it, p):
                    for g in range(G):
                        pool.wait_ge(scanned, it * G + g + 1)
                        if g == 0:
                            pool.wait_ge(item_read, it * NITEM + CI + 1)
                        ge(pool, y_done, it * 8 + (g - NHC) // 4 + 1)
                        pool.tensor_tensor(hc[:, g % NHC, :], hh[:, g % NHH, :], c_rep[:, p, :], ALU.mult).then_inc(hc_ready, 1)
                        prepare(it + 1, 1 - p, g)
                        if g == 22:
                            gate(it, p, 0)
                        if g == 6 and not (isinstance(it, int) and it == 0):
                            gate(it - 1, 1 - p, 1)

                def tail():
                    gate(NIT - 1, 1, 1)
                steps(pool, prepare, emit, tail)
        clear(nc, names)


def hilbert():
    s = np.zeros(W)
    s[1:W // 2], s[W // 2 + 1:] = 1, -1
    return np.real(np.fft.ifft(1j * s[:, None] * np.fft.fft(np.eye(W), axis=0), axis=0))


def host(i):
    f = np.float32
    c = np.ascontiguousarray
    w = {}
    w["win"] = c(i["L1_conv_in_proj_w"].T)
    w["taps"] = c(i["L1_conv_conv1d_w"][:, 0, :].T)
    xp = i["L1_conv_x_proj_w"]
    wx = np.zeros((128, 2, 128), f)
    wx[:, :, :40] = xp.reshape(40, 2, 128).transpose(2, 1, 0)
    w["wxd"] = wx
    wd = np.zeros((128, INNER), f)
    wd[:RANK] = i["L1_conv_dt_proj_w"].T
    w["wdt"] = wd
    p = np.arange(128)
    for name, off in (("sel_b", RANK), ("sel_c", RANK + ST)):
        m = np.zeros((128, 128), f)
        m[off + p % ST, p] = 1
        w[name] = m
    m = np.zeros((128, 8, 128), f)
    for j in range(8):
        for h in range(2):
            m[64 * h + 8 * j + p // ST, j, p] = 1
    w["sel_g"] = m.reshape(128, 1024)
    m = np.zeros((128, 4, 32), f)
    for j in range(4):
        m[p, j, 8 * j + p // ST] = 1
    w["sel_y"] = m
    w["wconv"] = c(i["L1_conv_conv_spatial_w"].reshape(C, C, 9).transpose(1, 2, 0))
    s = i["L1_conv_conv_spectral_w"][:, :, 0, 0].T
    w["wspec"] = c(np.stack([s[:C, :C], s[C:, :C], s[:C, C:], s[C:, C:]], 1))
    hm = hilbert()
    w["hilb"] = np.kron(np.eye(2), hm.T).astype(f)
    w["hil0"] = c(hm[:, 0][None]).astype(f)
    w["wout"] = c(i["L1_conv_out_proj_w"].reshape(C, 2, 128).transpose(2, 1, 0))
    two = lambda v: v.reshape(2, 128).T
    w["cols"] = c(np.concatenate([two(i["L1_conv_conv1d_b"]), two(i["L1_conv_dt_proj_b"]), two(i["L1_conv_D"]),
                                  i["L1_conv_conv_spatial_b"][:, None], two(i["L1_conv_conv_spectral_b"])], 1))
    w["a_log"] = c(i["L1_conv_A_log"].reshape(GROUPS, 128).T)
    return w


def build(nc, x, l0, w, out):
    z_ext = nc.dram_tensor("z_ext", [B, C, L + 2 * W], F32, kind="Internal").ap()
    layer0(nc, x, l0, z_ext)
    layer1(nc, z_ext, w, out)


def kernel(**inputs):
    import concourse.bacc as bacc
    from concourse.bass_utils import run_bass_kernel_spmd

    i = {k: np.asarray(v) for k, v in inputs.items()}
    l0 = {n: i["L0_conv_" + n] for n in ("Wq", "bq", "Wk", "bk", "Wv", "bv", "Wo", "bo", "gamma", "beta")}
    l0["ident"] = np.eye(128, dtype=np.float32)
    l0["sel_den"] = denominators()
    w = host(i)
    arrays = {"in_x": np.ascontiguousarray(i["x"].reshape(B, C, L))}
    arrays.update({"in_" + n: np.ascontiguousarray(v) for n, v in l0.items()})
    arrays.update({"in_" + n: np.ascontiguousarray(v) for n, v in w.items()})
    nc = bacc.Bacc("TRN2", target_bir_lowering=False, num_devices=1)
    aps = {n: nc.dram_tensor(n, v.shape, mybir.dt.from_np(v.dtype), kind="ExternalInput").ap() for n, v in arrays.items()}
    out = nc.dram_tensor("out", (B, C, L), F32, kind="ExternalOutput").ap()
    build(nc, aps["in_x"], {n: aps["in_" + n] for n in l0}, {n: aps["in_" + n] for n in w}, out)
    r = run_bass_kernel_spmd(nc, [arrays], core_ids=[0])
    return r.results[0]["out"].reshape(B, C, H, W)
```
